# Optimizing a Trainium2 kernel written in Bass

```python
import numpy as np
import jax
import jax.numpy as jnp

def _softmax(x, axis=-1):
    return jax.nn.softmax(x, axis=axis)

def _gelu(x):
    return jax.nn.gelu(x, approximate=True)

def _silu(x):
    return jax.nn.silu(x)

def _sigmoid(x):
    return jax.nn.sigmoid(x)

def _layernorm(x, axis=-1, eps=1e-05):
    m = jnp.mean(x, axis=axis, keepdims=True)
    v = jnp.var(x, axis=axis, keepdims=True)
    return (x - m) / jnp.sqrt(v + eps)

def _scatter_add(tgt, idx, src, axis=0):
    return tgt.at[idx].add(src)

def _segment_sum(src, seg, n):
    return jax.ops.segment_sum(src, seg, n)
kernel_name = 'mk_dlrm_tower_d1_rec_r8_291c66'

def setup_inputs(seed: int=0):
    np.random.seed(seed)
    _w = jnp.asarray

    def _rec_inputs():
        import jax
        import jax.numpy as jnp
        _tk = jax.random.key(seed)
        dense_ctx = jax.random.normal(jax.random.fold_in(_tk, 190), (512, 16), jnp.float32)
        ids = jnp.stack([jax.random.randint(jax.random.fold_in(_tk, 200 + f), (512,), 0, v, jnp.int32) for f, v in enumerate([12500, 12500, 1000, 1250, 12500, 125000, 1000, 1250, 1250, 1000, 1250, 1000, 12500, 12500, 12500, 1250, 1000, 12500, 1000, 125000, 12500, 1250, 12500, 125000, 125000, 1250, 1000, 1250, 1000, 1250, 125000, 1250, 12500, 125000, 1000, 1250, 125000, 12500, 12500])], axis=1)
        tbl_0 = 0.05 * jax.random.normal(jax.random.fold_in(_tk, 500 + 0), (12500, 16), jnp.float32)
        tbl_1 = 0.05 * jax.random.normal(jax.random.fold_in(_tk, 500 + 1), (12500, 16), jnp.float32)
        tbl_2 = 0.05 * jax.random.normal(jax.random.fold_in(_tk, 500 + 2), (1000, 16), jnp.float32)
        tbl_3 = 0.05 * jax.random.normal(jax.random.fold_in(_tk, 500 + 3), (1250, 16), jnp.float32)
        tbl_4 = 0.05 * jax.random.normal(jax.random.fold_in(_tk, 500 + 4), (12500, 16), jnp.float32)
        tbl_5 = 0.05 * jax.random.normal(jax.random.fold_in(_tk, 500 + 5), (125000, 16), jnp.float32)
        tbl_6 = 0.05 * jax.random.normal(jax.random.fold_in(_tk, 500 + 6), (1000, 16), jnp.float32)
        tbl_7 = 0.05 * jax.random.normal(jax.random.fold_in(_tk, 500 + 7), (1250, 16), jnp.float32)
        tbl_8 = 0.05 * jax.random.normal(jax.random.fold_in(_tk, 500 + 8), (1250, 16), jnp.float32)
        tbl_9 = 0.05 * jax.random.normal(jax.random.fold_in(_tk, 500 + 9), (1000, 16), jnp.float32)
        tbl_10 = 0.05 * jax.random.normal(jax.random.fold_in(_tk, 500 + 10), (1250, 16), jnp.float32)
        tbl_11 = 0.05 * jax.random.normal(jax.random.fold_in(_tk, 500 + 11), (1000, 16), jnp.float32)
        tbl_12 = 0.05 * jax.random.normal(jax.random.fold_in(_tk, 500 + 12), (12500, 16), jnp.float32)
        tbl_13 = 0.05 * jax.random.normal(jax.random.fold_in(_tk, 500 + 13), (12500, 16), jnp.float32)
        tbl_14 = 0.05 * jax.random.normal(jax.random.fold_in(_tk, 500 + 14), (12500, 16), jnp.float32)
        tbl_15 = 0.05 * jax.random.normal(jax.random.fold_in(_tk, 500 + 15), (1250, 16), jnp.float32)
        tbl_16 = 0.05 * jax.random.normal(jax.random.fold_in(_tk, 500 + 16), (1000, 16), jnp.float32)
        tbl_17 = 0.05 * jax.random.normal(jax.random.fold_in(_tk, 500 + 17), (12500, 16), jnp.float32)
        tbl_18 = 0.05 * jax.random.normal(jax.random.fold_in(_tk, 500 + 18), (1000, 16), jnp.float32)
        tbl_19 = 0.05 * jax.random.normal(jax.random.fold_in(_tk, 500 + 19), (125000, 16), jnp.float32)
        tbl_20 = 0.05 * jax.random.normal(jax.random.fold_in(_tk, 500 + 20), (12500, 16), jnp.float32)
        tbl_21 = 0.05 * jax.random.normal(jax.random.fold_in(_tk, 500 + 21), (1250, 16), jnp.float32)
        tbl_22 = 0.05 * jax.random.normal(jax.random.fold_in(_tk, 500 + 22), (12500, 16), jnp.float32)
        tbl_23 = 0.05 * jax.random.normal(jax.random.fold_in(_tk, 500 + 23), (125000, 16), jnp.float32)
        tbl_24 = 0.05 * jax.random.normal(jax.random.fold_in(_tk, 500 + 24), (125000, 16), jnp.float32)
        tbl_25 = 0.05 * jax.random.normal(jax.random.fold_in(_tk, 500 + 25), (1250, 16), jnp.float32)
        tbl_26 = 0.05 * jax.random.normal(jax.random.fold_in(_tk, 500 + 26), (1000, 16), jnp.float32)
        tbl_27 = 0.05 * jax.random.normal(jax.random.fold_in(_tk, 500 + 27), (1250, 16), jnp.float32)
        tbl_28 = 0.05 * jax.random.normal(jax.random.fold_in(_tk, 500 + 28), (1000, 16), jnp.float32)
        tbl_29 = 0.05 * jax.random.normal(jax.random.fold_in(_tk, 500 + 29), (1250, 16), jnp.float32)
        tbl_30 = 0.05 * jax.random.normal(jax.random.fold_in(_tk, 500 + 30), (125000, 16), jnp.float32)
        tbl_31 = 0.05 * jax.random.normal(jax.random.fold_in(_tk, 500 + 31), (1250, 16), jnp.float32)
        tbl_32 = 0.05 * jax.random.normal(jax.random.fold_in(_tk, 500 + 32), (12500, 16), jnp.float32)
        tbl_33 = 0.05 * jax.random.normal(jax.random.fold_in(_tk, 500 + 33), (125000, 16), jnp.float32)
        tbl_34 = 0.05 * jax.random.normal(jax.random.fold_in(_tk, 500 + 34), (1000, 16), jnp.float32)
        tbl_35 = 0.05 * jax.random.normal(jax.random.fold_in(_tk, 500 + 35), (1250, 16), jnp.float32)
        tbl_36 = 0.05 * jax.random.normal(jax.random.fold_in(_tk, 500 + 36), (125000, 16), jnp.float32)
        tbl_37 = 0.05 * jax.random.normal(jax.random.fold_in(_tk, 500 + 37), (12500, 16), jnp.float32)
        tbl_38 = 0.05 * jax.random.normal(jax.random.fold_in(_tk, 500 + 38), (12500, 16), jnp.float32)
        _rk = jax.random.fold_in(_tk, 7)
        W_top1 = 0.0606339 * jax.random.normal(jax.random.fold_in(_tk, 801), (272, 512), jnp.float32)
        W_top2 = 0.0441942 * jax.random.normal(jax.random.fold_in(_tk, 802), (512, 256), jnp.float32)
        W_top3 = 0.0625 * jax.random.normal(jax.random.fold_in(_tk, 803), (256, 1), jnp.float32)
        b_top1 = jnp.zeros((512,), jnp.float32)
        b_top2 = jnp.zeros((256,), jnp.float32)
        return (dense_ctx, ids, tbl_0, tbl_1, tbl_2, tbl_3, tbl_4, tbl_5, tbl_6, tbl_7, tbl_8, tbl_9, tbl_10, tbl_11, tbl_12, tbl_13, tbl_14, tbl_15, tbl_16, tbl_17, tbl_18, tbl_19, tbl_20, tbl_21, tbl_22, tbl_23, tbl_24, tbl_25, tbl_26, tbl_27, tbl_28, tbl_29, tbl_30, tbl_31, tbl_32, tbl_33, tbl_34, tbl_35, tbl_36, tbl_37, tbl_38, W_top1, b_top1, W_top2, b_top2, W_top3)
    dense_ctx, ids, tbl_0, tbl_1, tbl_2, tbl_3, tbl_4, tbl_5, tbl_6, tbl_7, tbl_8, tbl_9, tbl_10, tbl_11, tbl_12, tbl_13, tbl_14, tbl_15, tbl_16, tbl_17, tbl_18, tbl_19, tbl_20, tbl_21, tbl_22, tbl_23, tbl_24, tbl_25, tbl_26, tbl_27, tbl_28, tbl_29, tbl_30, tbl_31, tbl_32, tbl_33, tbl_34, tbl_35, tbl_36, tbl_37, tbl_38, W_top1, b_top1, W_top2, b_top2, W_top3 = _rec_inputs()

    def _L0_rec_setup():
        import jax, jax.numpy as jnp
        import numpy as np
        B, F0, D = (256, 39, 16)
        LAYER_SIZES = [128, 128, 128]
        key = jax.random.key(seed)
        ks = jax.random.split(key, 1 + 2 * len(LAYER_SIZES))
        inputs = jax.random.normal(ks[0], (B, F0, D), dtype=jnp.float32)
        out = {'inputs': inputs}
        field_nums = [F0]
        for i, size in enumerate(LAYER_SIZES):
            fk = field_nums[-1]
            fan_in = F0 * fk
            scale = np.sqrt(2.0 / (fan_in + size)).astype(np.float32)
            out[f'w{i}'] = jax.random.normal(ks[1 + 2 * i], (F0, fk, size), dtype=jnp.float32) * scale
            out[f'b{i}'] = jnp.zeros((size,), dtype=jnp.float32)
            field_nums.append(size // 2)
        return out
    _L0_rec_all = _L0_rec_setup()
    _L0_rec_in = {k: v for k, v in _L0_rec_all.items() if k in ('w0', 'w1', 'w2', 'b0', 'b1', 'b2')}
    del _L0_rec_all
    return {'dense_ctx': dense_ctx, 'ids': ids, 'tbl_0': tbl_0, 'tbl_1': tbl_1, 'tbl_2': tbl_2, 'tbl_3': tbl_3, 'tbl_4': tbl_4, 'tbl_5': tbl_5, 'tbl_6': tbl_6, 'tbl_7': tbl_7, 'tbl_8': tbl_8, 'tbl_9': tbl_9, 'tbl_10': tbl_10, 'tbl_11': tbl_11, 'tbl_12': tbl_12, 'tbl_13': tbl_13, 'tbl_14': tbl_14, 'tbl_15': tbl_15, 'tbl_16': tbl_16, 'tbl_17': tbl_17, 'tbl_18': tbl_18, 'tbl_19': tbl_19, 'tbl_20': tbl_20, 'tbl_21': tbl_21, 'tbl_22': tbl_22, 'tbl_23': tbl_23, 'tbl_24': tbl_24, 'tbl_25': tbl_25, 'tbl_26': tbl_26, 'tbl_27': tbl_27, 'tbl_28': tbl_28, 'tbl_29': tbl_29, 'tbl_30': tbl_30, 'tbl_31': tbl_31, 'tbl_32': tbl_32, 'tbl_33': tbl_33, 'tbl_34': tbl_34, 'tbl_35': tbl_35, 'tbl_36': tbl_36, 'tbl_37': tbl_37, 'tbl_38': tbl_38, 'W_top1': W_top1, 'b_top1': b_top1, 'W_top2': W_top2, 'b_top2': b_top2, 'W_top3': W_top3, 'L0_rec_w0': _L0_rec_in['w0'], 'L0_rec_w1': _L0_rec_in['w1'], 'L0_rec_w2': _L0_rec_in['w2'], 'L0_rec_b0': _L0_rec_in['b0'], 'L0_rec_b1': _L0_rec_in['b1'], 'L0_rec_b2': _L0_rec_in['b2']}

def reference(dense_ctx, ids, tbl_0, tbl_1, tbl_2, tbl_3, tbl_4, tbl_5, tbl_6, tbl_7, tbl_8, tbl_9, tbl_10, tbl_11, tbl_12, tbl_13, tbl_14, tbl_15, tbl_16, tbl_17, tbl_18, tbl_19, tbl_20, tbl_21, tbl_22, tbl_23, tbl_24, tbl_25, tbl_26, tbl_27, tbl_28, tbl_29, tbl_30, tbl_31, tbl_32, tbl_33, tbl_34, tbl_35, tbl_36, tbl_37, tbl_38, W_top1, b_top1, W_top2, b_top2, W_top3, L0_rec_w0, L0_rec_w1, L0_rec_w2, L0_rec_b0, L0_rec_b1, L0_rec_b2):
    import jax
    import jax.numpy as jnp

    def _L0_rec_ref(inputs, w0, w1, w2, b0, b1, b2):
        import jax, jax.numpy as jnp
        import numpy as np
        B, F0, D = (256, 39, 16)
        LAYER_SIZES = [128, 128, 128]
        x0 = inputs
        xk = inputs
        params = [(w0, b0), (w1, b1), (w2, b2)]
        n_layers = len(params)
        direct = []
        for idx, (W, b) in enumerate(params):
            z = jnp.einsum('bhd,bkd,hks->bsd', x0, xk, W) + b[None, :, None]
            z = jax.nn.relu(z)
            if idx != n_layers - 1:
                half = z.shape[1] // 2
                xk = z[:, :half, :]
                direct.append(z[:, half:, :])
            else:
                direct.append(z)
        logit = jnp.sum(jnp.concatenate(direct, axis=1), axis=-1)
        return logit
    e = jnp.stack([tbl_0[ids[:, 0]], tbl_1[ids[:, 1]], tbl_2[ids[:, 2]], tbl_3[ids[:, 3]], tbl_4[ids[:, 4]], tbl_5[ids[:, 5]], tbl_6[ids[:, 6]], tbl_7[ids[:, 7]], tbl_8[ids[:, 8]], tbl_9[ids[:, 9]], tbl_10[ids[:, 10]], tbl_11[ids[:, 11]], tbl_12[ids[:, 12]], tbl_13[ids[:, 13]], tbl_14[ids[:, 14]], tbl_15[ids[:, 15]], tbl_16[ids[:, 16]], tbl_17[ids[:, 17]], tbl_18[ids[:, 18]], tbl_19[ids[:, 19]], tbl_20[ids[:, 20]], tbl_21[ids[:, 21]], tbl_22[ids[:, 22]], tbl_23[ids[:, 23]], tbl_24[ids[:, 24]], tbl_25[ids[:, 25]], tbl_26[ids[:, 26]], tbl_27[ids[:, 27]], tbl_28[ids[:, 28]], tbl_29[ids[:, 29]], tbl_30[ids[:, 30]], tbl_31[ids[:, 31]], tbl_32[ids[:, 32]], tbl_33[ids[:, 33]], tbl_34[ids[:, 34]], tbl_35[ids[:, 35]], tbl_36[ids[:, 36]], tbl_37[ids[:, 37]], tbl_38[ids[:, 38]]], axis=1)
    z = _L0_rec_ref(e, L0_rec_w0, L0_rec_w1, L0_rec_w2, L0_rec_b0, L0_rec_b1, L0_rec_b2)
    z = z.reshape(z.shape[0], -1)
    h = jnp.concatenate([z, dense_ctx], axis=1)
    h = jnp.maximum(h @ W_top1 + b_top1, 0.0)
    h = jnp.maximum(h @ W_top2 + b_top2, 0.0)
    y = h @ W_top3
    return y

_drawn_inputs = setup_inputs


def setup_inputs(seed=0):
    import zlib

    import numpy as np

    out = dict(_drawn_inputs(seed))
    spreads = {'b_top1': (0.0, 2.0),
     'b_top2': (0.0, 2.0),
     'L0_rec_b0': (0.0, 0.354),
     'L0_rec_b1': (0.0, 0.519),
     'L0_rec_b2': (0.0, 0.8)}
    factors = {'tbl_0': 8.0,
     'tbl_1': 8.0,
     'tbl_2': 8.0,
     'tbl_3': 8.0,
     'tbl_4': 8.0,
     'tbl_5': 8.0,
     'tbl_6': 8.0,
     'tbl_7': 8.0,
     'tbl_8': 8.0,
     'tbl_9': 8.0,
     'tbl_10': 8.0,
     'tbl_11': 8.0,
     'tbl_12': 8.0,
     'tbl_13': 8.0,
     'tbl_14': 8.0,
     'tbl_15': 8.0,
     'tbl_16': 8.0,
     'tbl_17': 8.0,
     'tbl_18': 8.0,
     'tbl_19': 8.0,
     'tbl_20': 8.0,
     'tbl_21': 8.0,
     'tbl_22': 8.0,
     'tbl_23': 8.0,
     'tbl_24': 8.0,
     'tbl_25': 8.0,
     'tbl_26': 8.0,
     'tbl_27': 8.0,
     'tbl_28': 8.0,
     'tbl_29': 8.0,
     'tbl_30': 8.0,
     'tbl_31': 8.0,
     'tbl_32': 8.0,
     'tbl_33': 8.0,
     'tbl_34': 8.0,
     'tbl_35': 8.0,
     'tbl_36': 8.0,
     'tbl_37': 8.0,
     'tbl_38': 8.0,
     'L0_rec_w0': 8.0,
     'L0_rec_w1': 6.314,
     'L0_rec_w2': 4.985,
     'dense_ctx': 8.0}
    for name, (base, spread) in spreads.items():
        noise = np.random.default_rng([zlib.crc32(name.encode()), seed]).standard_normal(out[name].shape)
        drawn = base * np.exp(spread * noise) if base else spread * noise
        out[name] = jnp.asarray(drawn.astype(out[name].dtype))
    for name, factor in factors.items():
        out[name] = (out[name] * factor).astype(out[name].dtype)
    return out
```

```python
from contextlib import ExitStack

import numpy as np

import concourse.bass as bass
from concourse import mybir

P = 128
B = 512
F = 39
D = 16
S = 128
HALF = S // 2
DENSE = 16
H1, H2 = 512, 256
NBT = B // P
DC = 4
QPB = D // DC
N = DC * P
NCH = NBT * QPB
PARTS = 3
SR = PARTS * F

DELTAS = list(range(1, (F + 1) // 2)) + [0]
DPT = P // F
T0 = -(-len(DELTAS) // DPT)
R0 = DPT * F
R0_LAST = (len(DELTAS) - (T0 - 1) * DPT) * F
T1 = -(-F // 2)
R1_LAST = (F - (T1 - 1) * 2) * HALF
G0 = T0 // 2 + T0 % 2
G1 = T1 // 2
NSEL = 1 + T0 + T1

RING = 4
BC = 2
FIRST = G0 + G1
PER = G0 + 2 * G1
BPER = G0 + G1
assert PER % RING == 0 and BPER % BC == 0 and T1 % 2 == 0

ALU = mybir.AluOpType
ACT = mybir.ActivationFunctionType
AX = mybir.AxisListType
F32 = mybir.dt.float32
BF16 = mybir.dt.bfloat16
I32 = mybir.dt.int32


def group_no(i, kind, g):
    if kind == "L0":
        at = g
    elif kind == "L2":
        at = G0 + g
    else:
        at = G0 + G1 + g
    if isinstance(i, int) and i == 0:
        return (g if kind == "L0" else G0 + g) + 1
    if isinstance(i, int) and i == NCH:
        at = g
    return (i - 1) * PER + FIRST + at + 1


def slot(i, kind, g):
    return (group_no(i if isinstance(i, int) else 1, kind, g) - 1) % RING


def spread_no(i, kind, g):
    return i * BPER + (g if kind == "L0" else G0 + g) + 1


def tiles(kind, g):
    out = []
    last, full, end = (T0, R0, R0_LAST) if kind == "L0" else (T1, P, R1_LAST)
    for t in (2 * g, 2 * g + 1):
        if t < last:
            out.append((t, end if t == last - 1 else full))
    return out


def tower_kernel(nc, ids, tbls, sel, ident, w0a, w0b, w1, w2, biases, wt1, bt1, wt2, bt2, wt3, ctxT, out):
    with ExitStack() as ctx:
        def sb(name, shape, dt=F32):
            return ctx.enter_context(nc.sbuf_tensor(name, shape, dt))

        def psum(name, shape, dt=F32):
            return ctx.enter_context(nc.psum_tensor(name, shape, dt))

        def sem(name):
            return ctx.enter_context(nc.semaphore(name))

        ids_sb = sb("ids_sb", [P, NBT, F], I32)
        emb = sb("emb", [P, NBT, F, D])
        sel_sb = sb("sel_sb", [SR, NSEL, P], BF16)
        ident_sb = sb("ident_sb", [P, P], BF16)
        w0_sb = sb("w0_sb", [R0, T0, S])
        w0m_sb = sb("w0m_sb", [R0, T0, S])
        w1_sb = sb("w1_sb", [P, T1, S])
        w2_sb = sb("w2_sb", [P, T1, S])
        bias_sb = sb("bias_sb", [S, 3])
        part_f = sb("part_f", [P, 2, DC, F])
        parts = sb("parts", [P, DC, PARTS, F], BF16)
        xT = sb("xT", [SR, NCH, N], BF16)
        x0rep = sb("x0rep", [R0, N])
        spread = sb("spread", [P, T1, N])
        x1 = sb("x1", [P, N])
        x2 = sb("x2", [P, N])
        prod = sb("prod", [P, RING, 2, N])
        r01 = sb("r01", [P, N])
        r2 = sb("r2", [P, N])
        acc01 = sb("acc01", [P, NBT, N])
        acc2 = sb("acc2", [P, NBT, N])
        logit01 = sb("logit01", [P, B])
        logit2 = sb("logit2", [P, B])
        ctx_sb = sb("ctx_sb", [DENSE, B])
        wt1_sb = sb("wt1_sb", [P, 2, H1])
        wt1c_sb = sb("wt1c_sb", [DENSE, H1])
        bt1_sb = sb("bt1_sb", [P, H1 // P])
        wt2_sb = sb("wt2_sb", [P, H1 // P, H2])
        bt2_sb = sb("bt2_sb", [P, H2 // P])
        wt3_sb = sb("wt3_sb", [P, H2 // P])
        h1 = sb("h1", [P, H1 // P, B])
        h2 = sb("h2", [P, H2 // P, B])
        y_sb = sb("y_sb", [1, B])

        bc = psum("bc", [P, BC, 2, N])
        z0 = psum("z0", [P, N])
        z1 = psum("z1", [P, N])
        z2 = psum("z2", [P, N])
        aux = psum("aux", [P, N])
        auxT = aux[:, :].bitcast(BF16)

        ids_in = sem("ids_in")
        sel_in = sem("sel_in")
        w0_in = sem("w0_in")
        w1_in = sem("w1_in")
        w2_in = sem("w2_in")
        bias_in = sem("bias_in")
        top_in = sem("top_in")
        tile_in = [sem(f"tile_in{t}") for t in range(NBT)]
        gathered = sem("gathered")
        zeroed = sem("zeroed")
        w0_folded = sem("w0_folded")
        split = sem("split")
        transposed = sem("transposed")
        xT_ready = sem("xT_ready")
        base_done = sem("base_done")
        x0_ready = sem("x0_ready")
        spread_done = sem("spread_done")
        spread_kept = sem("spread_kept")
        prod_done = sem("prod_done")
        mm_done = sem("mm_done")
        x1_ready = sem("x1_ready")
        x2_ready = sem("x2_ready")
        r01_ready = sem("r01_ready")
        r2_ready = sem("r2_ready")
        r01_added = sem("r01_added")
        r2_added = sem("r2_added")
        logits_ready = sem("logits_ready")
        h1_done = sem("h1_done")
        h1_ready = sem("h1_ready")
        h2_done = sem("h2_done")
        h2_ready = sem("h2_ready")
        y_done = sem("y_done")
        y_ready = sem("y_ready")
        out_written = sem("out_written")

        block = ctx.enter_context(nc.Block())

        @block.sync
        def _(sp):
            sp.dma_start(ids_sb[:, :, :], ids.rearrange("(t p) f -> p t f", p=P)).then_inc(ids_in, 16)
            sp.dma_start(sel_sb[:, :, :], sel).then_inc(sel_in, 16)
            sp.dma_start(ident_sb[:, :], ident).then_inc(sel_in, 16)
            full0 = (T0 - 1) * R0
            sp.dma_start(w0_sb[:, 0:T0 - 1, :],
                         w0a[0:full0, :].rearrange("(t p) s -> p t s", p=R0)).then_inc(w0_in, 16)
            sp.dma_start(w0_sb[0:R0_LAST, T0 - 1, :], w0a[full0:, :]).then_inc(w0_in, 16)
            sp.dma_start(w0m_sb[:, 0:T0 - 1, :],
                         w0b[0:full0, :].rearrange("(t p) s -> p t s", p=R0)).then_inc(w0_in, 16)
            sp.wait_ge(zeroed, 1)
            sp.dma_start(w0m_sb[0:R0_LAST - F, T0 - 1, :], w0b[full0:, :]).then_inc(w0_in, 16)
            sp.dma_start(bias_sb[:, :], biases).then_inc(bias_in, 16)
            full1 = (T1 - 1) * P
            for w, w_sb, s in ((w1, w1_sb, w1_in), (w2, w2_sb, w2_in)):
                sp.dma_start(w_sb[:, 0:T1 - 1, :],
                             w[0:full1, :].rearrange("(t p) s -> p t s", p=P)).then_inc(s, 16)
                sp.dma_start(w_sb[0:R1_LAST, T1 - 1, :], w[full1:, :]).then_inc(s, 16)
            sp.dma_start(wt1_sb[:, :, :], wt1[0:2 * P, :].rearrange("(t p) n -> p t n", p=P)).then_inc(top_in, 16)
            sp.dma_start(wt1c_sb[:, :], wt1[2 * P:, :]).then_inc(top_in, 16)
            sp.dma_start(bt1_sb[:, :], bt1).then_inc(top_in, 16)
            sp.dma_start(wt2_sb[:, :, :], wt2.rearrange("(t p) n -> p t n", p=P)).then_inc(top_in, 16)
            sp.dma_start(bt2_sb[:, :], bt2).then_inc(top_in, 16)
            sp.dma_start(wt3_sb[:, :], wt3).then_inc(top_in, 16)
            sp.dma_start(ctx_sb[:, :], ctxT).then_inc(top_in, 16)
            sp.wait_ge(y_ready, 1)
            sp.dma_start(out.rearrange("b o -> o b"), y_sb[:, :]).then_inc(out_written, 16)
            sp.wait_ge(out_written, 16)

        @block.gpsimd
        def _(pool):
            pool.memset(w0m_sb[:, T0 - 1, :], 0.0).then_inc(zeroed, 1)
            pool.wait_ge(ids_in, 16)
            for t in range(NBT):
                for f in range(F):
                    pool.indirect_dma_start(
                        out=emb[:, t, f, :], out_offset=None, in_=tbls[f],
                        in_offset=bass.IndirectOffsetOnAxis(ap=ids_sb[:, t, f:f + 1], axis=0),
                    ).then_inc(tile_in[t], 16)
                pool.wait_ge(tile_in[t], 16 * F)
                pool.sem_inc(gathered, 1)

        @block.scalar
        def _(act):
            def take_xT(i):
                act.wait_ge(transposed, i + 1)
                act.activation(xT[:, bass.ds(i, 1), :].rearrange("p a n -> p (a n)"), auxT[0:SR, 0:N],
                               ACT.Copy).then_inc(xT_ready, 1)

            def take_base(i):
                act.wait_ge(base_done, i + 1)
                if not isinstance(i, int) or i >= 1:
                    act.wait_ge(prod_done, group_no(i - 1, "L0", G0 - 1))
                act.activation(x0rep[:, :], aux[0:R0, :], ACT.Copy).then_inc(x0_ready, 1)

            def keep_spread(i, g):
                act.wait_ge(spread_done, spread_no(i, "L1", g))
                if not isinstance(i, int) or i >= 1:
                    act.wait_ge(prod_done, group_no(i, "L2", g))
                act.activation(spread[:, 2 * g:2 * g + 2, :], bc[:, (G0 + g) % BC, :, :],
                               ACT.Copy).then_inc(spread_kept, 1)

            def relu0(i):
                act.wait_ge(mm_done, group_no(i, "L0", G0 - 1))
                if not isinstance(i, int) or i >= 1:
                    act.wait_ge(prod_done, group_no(i - 1, "L1", G1 - 1))
                    act.wait_ge(r01_added, i)
                act.activation(x1[0:HALF, :], z0[0:HALF, :], ACT.Relu,
                               bias=bias_sb[0:HALF, 0:1]).then_inc(x1_ready, 1)
                act.activation(x1[HALF:S, :], z0[0:HALF, :], ACT.Relu,
                               bias=bias_sb[0:HALF, 0:1]).then_inc(x1_ready, 1)
                act.activation(r01[HALF:S, :], z0[HALF:S, :], ACT.Relu,
                               bias=bias_sb[HALF:S, 0:1]).then_inc(r01_ready, 1)

            def relu1(i):
                act.wait_ge(mm_done, group_no(i, "L1", G1 - 1))
                act.activation(x2[0:HALF, :], z1[HALF:S, :], ACT.Relu,
                               bias=bias_sb[HALF:S, 1:2]).then_inc(x2_ready, 1)
                act.activation(x2[HALF:S, :], z1[HALF:S, :], ACT.Relu,
                               bias=bias_sb[HALF:S, 1:2]).then_inc(x2_ready, 1)
                act.activation(r01[0:HALF, :], z1[0:HALF, :], ACT.Relu,
                               bias=bias_sb[0:HALF, 1:2]).then_inc(r01_ready, 1)

            def relu2(i):
                act.wait_ge(mm_done, group_no(i + 1, "L2", G1 - 1))
                if not isinstance(i, int) or i >= 1:
                    act.wait_ge(r2_added, i)
                act.activation(r2[:, :], z2[:, :], ACT.Relu, bias=bias_sb[:, 2:3]).then_inc(r2_ready, 1)

            def one_pass(i, first=False, last=False):
                relu0(i)
                for g in range(G1):
                    keep_spread(i, g)
                    if g == 0 and not first:
                        relu2(i - 1)
                    if g == 3 and not last:
                        take_xT(i + 1)
                    if g == 4 and not last:
                        take_base(i + 1)
                relu1(i)

            take_xT(0)
            take_base(0)
            act.wait_ge(bias_in, 16)
            one_pass(0, first=True)
            with act.Fori(1, NCH - 1) as i:
                one_pass(i)
            one_pass(NCH - 1, last=True)
            relu2(NCH - 1)

            act.wait_ge(top_in, 16 * 7)
            for m in range(H1 // P):
                act.wait_ge(h1_done, m + 1)
                act.activation(h1[:, m, :], bc[:, m // 2, m % 2, :], ACT.Relu,
                               bias=bt1_sb[:, m:m + 1]).then_inc(h1_ready, 1)
            for m in range(H2 // P):
                act.wait_ge(h2_done, m + 1)
                act.activation(h2[:, m, :], (z0, z1)[m][:, :], ACT.Relu,
                               bias=bt2_sb[:, m:m + 1]).then_inc(h2_ready, 1)
            act.wait_ge(y_done, 1)
            act.activation(y_sb[:, :], z2[0:1, :], ACT.Copy).then_inc(y_ready, 1)

        @block.vector
        def _(dve):
            def split_chunk(i):
                dve.wait_ge(gathered, (i // QPB) + 1)
                if not isinstance(i, int) or i >= 1:
                    dve.wait_ge(transposed, i)
                src = emb[:, bass.ds(i // QPB, 1), :, bass.ds((i % QPB) * DC, DC)].rearrange("p a f d -> p (a d) f")
                rest, rest2 = part_f[:, 0, :, :], part_f[:, 1, :, :]
                dve.tensor_copy(parts[:, :, 0, :], src).then_inc(split, 1)
                dve.wait_ge(split, i * 4 + 1)
                dve.tensor_tensor(rest, src, parts[:, :, 0, :], ALU.subtract).then_inc(split, 1)
                dve.wait_ge(split, i * 4 + 2)
                dve.tensor_copy(parts[:, :, 1, :], rest).then_inc(split, 1)
                dve.wait_ge(split, i * 4 + 3)
                dve.tensor_tensor(parts[:, :, 2, :], rest, parts[:, :, 1, :], ALU.subtract).then_inc(split, 1)

            def free_slot(i, kind, g):
                n = group_no(i, kind, g)
                if not isinstance(n, int) or n > RING:
                    dve.wait_ge(mm_done, n - RING)

            def product0(i, g):
                dve.wait_ge(spread_done, spread_no(i, "L0", g))
                if g == 0:
                    dve.wait_ge(x0_ready, i + 1)
                free_slot(i, "L0", g)
                k, rows = len(tiles("L0", g)), tiles("L0", g)[0][1]
                dve.tensor_tensor(prod[0:rows, slot(i, "L0", g), 0:k, :], bc[0:rows, g % BC, 0:k, :],
                                  x0rep[0:rows, :].unsqueeze(1).to_broadcast([rows, k, N]),
                                  ALU.mult).then_inc(prod_done, 1)

            def product1(i, g):
                if g == 0:
                    dve.wait_ge(x1_ready, 2 * (i + 1))
                dve.wait_ge(spread_kept, i * G1 + g + 1)
                free_slot(i, "L1", g)
                dve.tensor_tensor(prod[:, slot(i, "L1", g), :, :], spread[:, 2 * g:2 * g + 2, :],
                                  x1[:, :].unsqueeze(1).to_broadcast([P, 2, N]),
                                  ALU.mult).then_inc(prod_done, 1)

            def product2(i, g):
                if g == 0:
                    dve.wait_ge(x2_ready, 2 * (i + 1))
                dve.wait_ge(spread_kept, i * G1 + g + 1)
                free_slot(i + 1, "L2", g)
                dve.tensor_tensor(prod[:, slot(i + 1, "L2", g), :, :], spread[:, 2 * g:2 * g + 2, :],
                                  x2[:, :].unsqueeze(1).to_broadcast([P, 2, N]),
                                  ALU.mult).then_inc(prod_done, 1)

            def add01(i):
                dve.wait_ge(r01_ready, 2 * (i + 1))
                a = acc01[:, bass.ds(i // QPB, 1), :].rearrange("p a n -> p (a n)")
                dve.tensor_tensor(a, a, r01[:, :], ALU.add).then_inc(r01_added, 1)

            def add2(i):
                dve.wait_ge(r2_ready, i + 1)
                a = acc2[:, bass.ds(i // QPB, 1), :].rearrange("p a n -> p (a n)")
                dve.tensor_tensor(a, a, r2[:, :], ALU.add).then_inc(r2_added, 1)

            def one_pass(i, first=False, last=False):
                for g in range(G0):
                    product0(i, g)
                if not first:
                    add01(i - 1)
                    for g in range(G1):
                        product2(i - 1, g)
                for g in range(G1):
                    product1(i, g)
                    if g == 0 and not last:
                        split_chunk(i + 1)
                    if g == 3 and not first:
                        add2(i - 1)

            dve.memset(acc01[:, :, :], 0.0)
            dve.memset(acc2[:, :, :], 0.0)
            dve.wait_ge(w0_in, 16 * 4)
            for t in range(T0):
                r = R0_LAST if t == T0 - 1 else R0
                dve.tensor_tensor(w0_sb[0:r, t, :], w0_sb[0:r, t, :], w0m_sb[0:r, t, :], ALU.add
                                  ).then_inc(w0_folded, 1)
            split_chunk(0)
            one_pass(0, first=True)
            with dve.Fori(1, NCH - 1) as i:
                one_pass(i)
            one_pass(NCH - 1, last=True)
            add01(NCH - 1)
            for g in range(G1):
                product2(NCH - 1, g)
            dve.wait_ge(r01_added, NCH)
            dve.tensor_reduce(logit01[:, :].rearrange("p (t b) -> p t b", b=P),
                              acc01[:, :, :].rearrange("p t (d b) -> p t b d", d=DC), AX.X, ALU.add
                              ).then_inc(logits_ready, 1)
            add2(NCH - 1)
            dve.wait_ge(r2_added, NCH)
            dve.tensor_reduce(logit2[:, :].rearrange("p (t b) -> p t b", b=P),
                              acc2[:, :, :].rearrange("p t (d b) -> p t b d", d=DC), AX.X, ALU.add
                              ).then_inc(logits_ready, 1)

        @block.tensor
        def _(pe):
            def turn(i):
                pe.wait_ge(split, 4 * (i + 1))
                if not isinstance(i, int) or i >= 1:
                    pe.wait_ge(x0_ready, i)
                for d in range(DC):
                    last = pe.transpose(auxT[0:SR, d * P:(d + 1) * P],
                                        parts[:, d, :, :].rearrange("p a f -> p (a f)"), ident_sb[:, :])
                last.then_inc(transposed, 1)

            def chosen(i, m, rows, dst):
                return pe.matmul(dst, sel_sb[:, m, 0:rows],
                                 xT[:, bass.ds(i, 1), :].rearrange("p a n -> p (a n)"), start=True, stop=True)

            def base(i):
                pe.wait_ge(xT_ready, i + 1)
                chosen(i, 0, R0, aux[0:R0, :]).then_inc(base_done, 1)

            def spread_rows(i, kind, g):
                n = spread_no(i, kind, g)
                b = (n - 1) % BC if isinstance(n, int) else ((g if kind == "L0" else G0 + g) % BC)
                if kind == "L0" and g < BC:
                    if not isinstance(i, int) or i >= 1:
                        pe.wait_ge(spread_kept, i * G1 - BC + g + 1)
                elif kind == "L0":
                    pe.wait_ge(prod_done, group_no(i, "L0", g - BC))
                elif g < BC:
                    pe.wait_ge(prod_done, group_no(i, "L0", G0 - BC + g))
                else:
                    pe.wait_ge(spread_kept, i * G1 + g - BC + 1)
                for j, (t, rows) in enumerate(tiles(kind, g)):
                    m = 1 + t + (T0 if kind == "L1" else 0)
                    cols = rows if kind == "L0" else P
                    last = chosen(i, m, cols, bc[0:cols, b, j, :])
                last.then_inc(spread_done, 1)

            def sum_group(i, kind, g):
                pe.wait_ge(prod_done, group_no(i, kind, g))
                z, w = {"L0": (z0, w0_sb), "L1": (z1, w1_sb), "L2": (z2, w2_sb)}[kind]
                if g == 0 and (not isinstance(i, int) or i >= 1):
                    if kind == "L0":
                        pe.wait_ge(x1_ready, 2 * i)
                        pe.wait_ge(r01_ready, 2 * i - 1)
                    elif kind == "L1":
                        pe.wait_ge(x2_ready, 2 * i)
                        pe.wait_ge(r01_ready, 2 * i)
                    elif not isinstance(i, int) or i >= 2:
                        pe.wait_ge(r2_ready, i - 1)
                count = T0 if kind == "L0" else T1
                for j, (t, rows) in enumerate(tiles(kind, g)):
                    last = pe.matmul(z[:, :], w[0:rows, t, :], prod[0:rows, slot(i, kind, g), j, :],
                                     start=(t == 0), stop=(t == count - 1))
                last.then_inc(mm_done, 1)

            def one_pass(i, first=False, last=False):
                for g in range(G0):
                    sum_group(i, "L0", g)
                    if g + BC < G0:
                        spread_rows(i, "L0", g + BC)
                    else:
                        spread_rows(i, "L1", g + BC - G0)
                if first:
                    pe.wait_ge(w1_in, 32)
                    pe.wait_ge(w2_in, 32)
                else:
                    for g in range(G1):
                        sum_group(i, "L2", g)
                for g in range(G1):
                    sum_group(i, "L1", g)
                    if g + BC < G1:
                        spread_rows(i, "L1", g + BC)
                    elif not last:
                        spread_rows(i + 1, "L0", g + BC - G1)
                    if g == 2 and not last:
                        turn(i + 1)
                    if g == 3 and not last:
                        base(i + 1)

            pe.wait_ge(sel_in, 32)
            turn(0)
            base(0)
            for g in range(BC):
                spread_rows(0, "L0", g)
            pe.wait_ge(w0_folded, T0)
            one_pass(0, first=True)
            with pe.Fori(1, NCH - 1) as i:
                one_pass(i)
            one_pass(NCH - 1, last=True)
            for g in range(G1):
                sum_group(NCH, "L2", g)

            pe.wait_ge(top_in, 16 * 7)
            pe.wait_ge(logits_ready, 2)
            for m in range(H1 // P):
                o = bc[:, m // 2, m % 2, :]
                cols = slice(m * P, (m + 1) * P)
                pe.matmul(o, wt1c_sb[:, cols], ctx_sb[:, :], start=True, stop=False)
                pe.matmul(o, wt1_sb[:, 0, cols], logit01[:, :], start=False, stop=False)
                pe.matmul(o, wt1_sb[:, 1, cols], logit2[:, :], start=False, stop=True).then_inc(h1_done, 1)
            for m in range(H2 // P):
                for k in range(H1 // P):
                    if m == 0:
                        pe.wait_ge(h1_ready, k + 1)
                    last = pe.matmul((z0, z1)[m][:, :], wt2_sb[:, k, m * P:(m + 1) * P], h1[:, k, :],
                                     start=(k == 0), stop=(k == H1 // P - 1))
                last.then_inc(h2_done, 1)
            for k in range(H2 // P):
                pe.wait_ge(h2_ready, k + 1)
                last = pe.matmul(z2[0:1, :], wt3_sb[:, k:k + 1], h2[:, k, :],
                                 start=(k == 0), stop=(k == H2 // P - 1))
            last.then_inc(y_done, 1)


def selection(bf16):
    take = np.zeros((NSEL, P), np.int64)
    take[0, :] = np.arange(P) % F
    for t in range(T0):
        for j in range(DPT):
            n = t * DPT + j
            if n < len(DELTAS):
                take[1 + t, j * F:(j + 1) * F] = (np.arange(F) + DELTAS[n]) % F
    for t in range(T1):
        take[1 + T0 + t, :] = np.minimum(2 * t + np.arange(P) // HALF, F - 1)
    rows = np.arange(SR) % F
    return (rows[:, None, None] == take[None, :, :]).astype(bf16)


def kernel(**inputs):
    import ml_dtypes
    import concourse.bacc as bacc
    from concourse.bass_utils import run_bass_kernel_spmd

    a = {k: np.asarray(v) for k, v in inputs.items()}
    bf16 = ml_dtypes.bfloat16
    fields = np.arange(F)
    h_of = np.concatenate([fields for _ in DELTAS])
    k_of = np.concatenate([(fields + d) % F for d in DELTAS])
    mirrored = (len(DELTAS) - 1) * F
    swap = np.concatenate([np.arange(HALF, S), np.arange(HALF)])
    wt1 = a["W_top1"]
    arrays = {
        "ids": a["ids"],
        "sel": selection(bf16),
        "ident": np.eye(P).astype(bf16),
        "w0a": a["L0_rec_w0"][h_of, k_of],
        "w0b": a["L0_rec_w0"][k_of, h_of][:mirrored],
        "w1": a["L0_rec_w1"].reshape(F * HALF, S)[:, swap],
        "w2": a["L0_rec_w2"].reshape(F * HALF, S),
        "biases": np.stack([a["L0_rec_b0"], a["L0_rec_b1"][swap], a["L0_rec_b2"]], axis=1),
        "wt1": np.concatenate([wt1[HALF:S], wt1[:HALF], wt1[S:]], axis=0),
        "bt1": a["b_top1"].reshape(-1, P).T,
        "wt2": a["W_top2"],
        "bt2": a["b_top2"].reshape(-1, P).T,
        "wt3": a["W_top3"].reshape(-1, P).T,
        "ctxT": a["dense_ctx"].T,
    }
    for f in range(F):
        arrays[f"tbl_{f}"] = a[f"tbl_{f}"]
    arrays = {f"{k}_dram": np.ascontiguousarray(v) for k, v in arrays.items()}
    nc = bacc.Bacc("TRN2", target_bir_lowering=False, num_devices=1)
    ap = {k: nc.dram_tensor(k, v.shape, mybir.dt.from_np(v.dtype), kind="ExternalInput").ap()
          for k, v in arrays.items()}
    out = nc.dram_tensor("out_dram", (B, 1), F32, kind="ExternalOutput").ap()
    tower_kernel(nc, ap["ids_dram"], [ap[f"tbl_{f}_dram"] for f in range(F)],
                 *[ap[f"{k}_dram"] for k in ("sel", "ident", "w0a", "w0b", "w1", "w2", "biases",
                                             "wt1", "bt1", "wt2", "bt2", "wt3", "ctxT")], out)
    r = run_bass_kernel_spmd(nc, [arrays], core_ids=[0])
    return r.results[0]["out_dram"]
```

```python
from contextlib import ExitStack

import numpy as np

import concourse.bass as bass
from concourse import mybir

P = 128
B = 512
F = 39
D = 16
S = 128
HALF = S // 2
DENSE = 16
H1, H2 = 512, 256
NBT = B // P
DC = 4
QPB = D // DC
N = DC * P
NCH = NBT * QPB
PARTS = 3
SR = PARTS * F

DELTAS = list(range(1, (F + 1) // 2)) + [0]
DPT = P // F
T0 = -(-len(DELTAS) // DPT)
R0 = DPT * F
R0_LAST = (len(DELTAS) - (T0 - 1) * DPT) * F
T1 = -(-F // 2)
R1_LAST = (F - (T1 - 1) * 2) * HALF
G0 = T0 // 2 + T0 % 2
G1 = T1 // 2
NSEL = 1 + T0

RING = 4
HRING = 2
BC = 2
LAG = 2

L0S = [("L0", g) for g in range(G0)]
L1S = [("L1", g) for g in range(G1)]
L2S = [("L2", g) for g in range(G1)]
FIRST, EVERY = L0S + L1S, L0S + L2S + L1S
PIECE = 2
PIECES = G1 // PIECE

SPLIT = {"L0": (0, 3), "L2": (2, 5, 8), "L1": (1, 4, 7)}

ALU = mybir.AluOpType
ACT = mybir.ActivationFunctionType
AX = mybir.AxisListType
F32 = mybir.dt.float32
F32R = mybir.dt.float32r
BF16 = mybir.dt.bfloat16
I32 = mybir.dt.int32


def is_split(kind, g):
    return g in SPLIT[kind]


def known(i, least):
    return not isinstance(i, int) or i >= least


def number(i, kind, g, split_only=False):
    def count(groups):
        return sum(1 for x in groups if is_split(*x) or not split_only)
    if isinstance(i, int) and i == 0:
        return count(FIRST[:FIRST.index((kind, g)) + 1])
    order = L2S if isinstance(i, int) and i == NCH else EVERY
    return (i - 1) * count(EVERY) + count(FIRST) + count(order[:order.index((kind, g)) + 1])


def before(i, kind, g, back, split_only=False):
    def some(groups):
        return [x for x in groups if is_split(*x) or not split_only]
    order = FIRST if isinstance(i, int) and i == 0 else L2S if isinstance(i, int) and i == NCH else EVERY
    at = some(order).index((kind, g)) - back
    if at >= 0:
        return (i, *some(order)[at])
    if not known(i, 1):
        return None
    assert some(FIRST)[at] == some(EVERY)[at]
    return (i - 1, *some(EVERY)[at])


def slot(i, kind, g):
    return (number(i if isinstance(i, int) else 1, kind, g) - 1) % RING


def split_slot(i, kind, g):
    return (number(i if isinstance(i, int) else 1, kind, g, True) - 1) % HRING


assert len(EVERY) % RING == 0 and G0 % BC == 0 and T1 % 2 == 0 and G1 % PIECE == 0
assert sum(is_split(*x) for x in EVERY) % HRING == 0
assert not any(is_split(*x) for x in EVERY[-LAG:])


def tiles(kind, g):
    out = []
    last, full, end = (T0, R0, R0_LAST) if kind == "L0" else (T1, P, R1_LAST)
    for t in (2 * g, 2 * g + 1):
        if t < last:
            out.append((t, end if t == last - 1 else full))
    return out


def tower_kernel(nc, ids, tbls, sel, ident, w0a, w0b, w1, w2, biases, wt1, bt1, wt2, bt2, wt3, ctxT, out):
    with ExitStack() as ctx:
        def sb(name, shape, dt=F32):
            return ctx.enter_context(nc.sbuf_tensor(name, shape, dt))

        def psum(name, shape, dt=F32):
            return ctx.enter_context(nc.psum_tensor(name, shape, dt))

        def sem(name):
            return ctx.enter_context(nc.semaphore(name))

        ids_sb = sb("ids_sb", [P, NBT, F], I32)
        emb = sb("emb", [P, NBT, F, D])
        sel_sb = sb("sel_sb", [SR, NSEL, P], BF16)
        ident_sb = sb("ident_sb", [P, P], BF16)
        w0_sb = sb("w0_sb", [R0, T0, S])
        w0m_sb = sb("w0m_sb", [R0, T0, S])
        w1_sb = sb("w1_sb", [P, T1, S])
        w2_sb = sb("w2_sb", [P, T1, S])
        high_w = {k: sb(f"high_w_{k}", [P, len(SPLIT[k]), 2, S], F32R) for k in SPLIT}
        low_w = {k: sb(f"low_w_{k}", [P, len(SPLIT[k]), 2, S], F32R) for k in SPLIT}
        bias_sb = sb("bias_sb", [S, 3])
        rest = sb("rest", [P, DC, F])
        parts = sb("parts", [P, DC, PARTS, F], BF16)
        xT = sb("xT", [SR, 2, N], BF16)
        x0rep = sb("x0rep", [R0, N])
        spread = sb("spread", [P, T1, N])
        x0_dram = nc.dram_tensor("x0_rows", [NCH, F, N], F32, kind="Internal")
        x1 = sb("x1", [P, N])
        x2 = sb("x2", [P, N])
        prod = sb("prod", [P, RING, 2, N])
        high = sb("high", [P, HRING, 2, N], F32R)
        low = sb("low", [P, HRING, 2, N], F32R)
        r01 = sb("r01", [P, N])
        r2 = sb("r2", [P, N])
        acc01 = sb("acc01", [P, NBT, N])
        acc2 = sb("acc2", [P, NBT, N])
        ctx_sb = sb("ctx_sb", [DENSE, B])
        wt1_sb = sb("wt1_sb", [P, 2, H1])
        wt1c_sb = sb("wt1c_sb", [DENSE, H1])
        bt1_sb = sb("bt1_sb", [P, H1 // P])
        wt2_sb = sb("wt2_sb", [P, H1 // P, H2])
        bt2_sb = sb("bt2_sb", [P, H2 // P])
        wt3_sb = sb("wt3_sb", [P, H2 // P])
        y_sb = sb("y_sb", [1, B])
        logit01, logit2 = spread[:, 0, :], spread[:, 1, :]
        h1 = spread[:, 2:2 + H1 // P, :]
        h2 = spread[:, 2 + H1 // P:2 + H1 // P + H2 // P, :]

        bc = psum("bc", [P, BC, 2, N])
        z0 = psum("z0", [P, N])
        z1 = psum("z1", [P, N])
        z2 = psum("z2", [P, N])
        aux = psum("aux", [P, N])
        auxT = aux[:, :].bitcast(BF16)

        def x0_of(i):
            return emb[:, bass.ds(i // QPB, 1), :, bass.ds((i % QPB) * DC, DC)].rearrange("p a f d -> p (a d) f")

        ids_in = sem("ids_in")
        sel_in = sem("sel_in")
        w0_in = sem("w0_in")
        w1_in = sem("w1_in")
        w2_in = sem("w2_in")
        bias_in = sem("bias_in")
        top_in = sem("top_in")
        tile_in = [sem(f"tile_in{t}") for t in range(NBT)]
        gathered = sem("gathered")
        zeroed = sem("zeroed")
        edge_zeroed = sem("edge_zeroed")
        w0_folded = sem("w0_folded")
        high_w_ready = sem("high_w_ready")
        low_w_ready = sem("low_w_ready")
        part0_ready = sem("part0_ready")
        rest_ready = sem("rest_ready")
        part1_ready = sem("part1_ready")
        split = sem("split")
        transposed = sem("transposed")
        xT_ready = sem("xT_ready")
        base_done = sem("base_done")
        x0_ready = sem("x0_ready")
        x0_stored = sem("x0_stored")
        spread_in = [sem(f"spread_in{p}") for p in range(PIECES)]
        spread_done = sem("spread_done")
        prod_done = sem("prod_done")
        high_ready = sem("high_ready")
        low_ready = sem("low_ready")
        mm_done = sem("mm_done")
        x1_ready = sem("x1_ready")
        x2_ready = sem("x2_ready")
        r01_ready = sem("r01_ready")
        r2_ready = sem("r2_ready")
        r01_added = sem("r01_added")
        r2_added = sem("r2_added")
        logits_ready = sem("logits_ready")
        h1_done = sem("h1_done")
        h1_ready = sem("h1_ready")
        h2_done = sem("h2_done")
        h2_ready = sem("h2_ready")
        y_done = sem("y_done")
        y_ready = sem("y_ready")
        out_written = sem("out_written")

        block = ctx.enter_context(nc.Block())

        @block.sync
        def _(sp):
            sp.dma_start(ids_sb[:, :, :], ids.rearrange("(t p) f -> p t f", p=P)).then_inc(ids_in, 16)
            sp.dma_start(sel_sb[:, :, :], sel).then_inc(sel_in, 16)
            sp.dma_start(ident_sb[:, :], ident).then_inc(sel_in, 16)
            full0 = (T0 - 1) * R0
            sp.dma_start(w0_sb[:, 0:T0 - 1, :],
                         w0a[0:full0, :].rearrange("(t p) s -> p t s", p=R0)).then_inc(w0_in, 16)
            sp.dma_start(w0_sb[0:R0_LAST, T0 - 1, :], w0a[full0:, :]).then_inc(w0_in, 16)
            sp.dma_start(w0m_sb[:, 0:T0 - 1, :],
                         w0b[0:full0, :].rearrange("(t p) s -> p t s", p=R0)).then_inc(w0_in, 16)
            sp.wait_ge(zeroed, 1)
            sp.dma_start(w0m_sb[0:R0_LAST - F, T0 - 1, :], w0b[full0:, :]).then_inc(w0_in, 16)
            sp.dma_start(bias_sb[:, :], biases).then_inc(bias_in, 16)
            full1 = (T1 - 1) * P
            for w, w_sb, s in ((w1, w1_sb, w1_in), (w2, w2_sb, w2_in)):
                sp.dma_start(w_sb[:, 0:T1 - 1, :],
                             w[0:full1, :].rearrange("(t p) s -> p t s", p=P)).then_inc(s, 16)
                sp.dma_start(w_sb[0:R1_LAST, T1 - 1, :], w[full1:, :]).then_inc(s, 16)
            sp.dma_start(wt1_sb[:, :, :], wt1[0:2 * P, :].rearrange("(t p) n -> p t n", p=P)).then_inc(top_in, 16)
            sp.dma_start(wt1c_sb[:, :], wt1[2 * P:, :]).then_inc(top_in, 16)
            sp.dma_start(bt1_sb[:, :], bt1).then_inc(top_in, 16)
            sp.dma_start(wt2_sb[:, :, :], wt2.rearrange("(t p) n -> p t n", p=P)).then_inc(top_in, 16)
            sp.dma_start(bt2_sb[:, :], bt2).then_inc(top_in, 16)
            sp.dma_start(wt3_sb[:, :], wt3).then_inc(top_in, 16)
            sp.dma_start(ctx_sb[:, :], ctxT).then_inc(top_in, 16)

            def store_x0(i):
                sp.wait_ge(x0_ready, i + 1)
                sp.dma_start(x0_dram[bass.ds(i, 1), :, :].rearrange("a f n -> (a f) n"),
                             x0rep[0:F, :]).then_inc(x0_stored, 16)

            def spread_piece(i, p):
                if known(i, 1):
                    sp.wait_ge(prod_done, number(i, "L2", PIECE * (p + 1) - 1))
                if p == 0:
                    sp.wait_ge(x0_stored, 16 * (i + 1))
                for half in range(2):
                    t = 2 * PIECE * p
                    many = len(range(2 * t + half, min(F, 2 * t + 4 * PIECE), 2))
                    src = x0_dram[bass.ds(i, 1), bass.ds(2 * t + half, many, 2), :].rearrange("a f n -> (a f) n")
                    sp.dma_start(spread[half * HALF:(half + 1) * HALF, t:t + many, :],
                                 src.unsqueeze(0).to_broadcast([HALF, many, N])).then_inc(spread_in[p], 16)

            store_x0(0)
            sp.wait_ge(edge_zeroed, 1)
            for p in range(PIECES):
                spread_piece(0, p)
            store_x0(1)
            with sp.Fori(1, NCH - 1) as i:
                for p in range(PIECES):
                    spread_piece(i, p)
                store_x0(i + 1)
            for p in range(PIECES):
                spread_piece(NCH - 1, p)

            sp.wait_ge(y_ready, 1)
            sp.dma_start(out.rearrange("b o -> o b"), y_sb[:, :]).then_inc(out_written, 16)
            sp.wait_ge(out_written, 16)

        @block.gpsimd
        def _(pool):
            pool.memset(w0m_sb[:, T0 - 1, :], 0.0).then_inc(zeroed, 1)
            pool.wait_ge(zeroed, 1)
            pool.memset(spread[HALF:P, T1 - 1, :], 0.0).then_inc(edge_zeroed, 1)
            pool.wait_ge(edge_zeroed, 1)
            pool.wait_ge(ids_in, 16)
            for t in range(NBT):
                for f in range(F):
                    pool.indirect_dma_start(
                        out=emb[:, t, f, :], out_offset=None, in_=tbls[f],
                        in_offset=bass.IndirectOffsetOnAxis(ap=ids_sb[:, t, f:f + 1], axis=0),
                    ).then_inc(tile_in[t], 16)
                pool.wait_ge(tile_in[t], 16 * F)
                pool.sem_inc(gathered, 1)

        @block.scalar
        def _(act):
            def split_weights(kind, w):
                for n, g in enumerate(SPLIT[kind]):
                    for j, (t, rows) in enumerate(tiles(kind, g)):
                        last = act.activation(high_w[kind][0:rows, n, j, :], w[0:rows, t, :], ACT.Copy)
                last.then_inc(high_w_ready, 1)

            def take_xT(i):
                act.wait_ge(transposed, i + 1)
                act.activation(xT[:, bass.ds(i % 2, 1), :].rearrange("p a n -> p (a n)"), auxT[0:SR, 0:N],
                               ACT.Copy).then_inc(xT_ready, 1)

            def take_base(i):
                act.wait_ge(base_done, i + 1)
                if known(i, 1):
                    act.wait_ge(prod_done, number(i - 1, "L0", G0 - 1))
                    act.wait_ge(x0_stored, 16 * i)
                act.activation(x0rep[:, :], aux[0:R0, :], ACT.Copy).then_inc(x0_ready, 1)

            def take_part0(i):
                act.wait_ge(gathered, (i // QPB) + 1)
                if known(i, 1):
                    act.wait_ge(transposed, i)
                act.activation(parts[:, :, 0, :], x0_of(i), ACT.Copy).then_inc(part0_ready, 1)

            def take_part1(i):
                act.wait_ge(rest_ready, i + 1)
                act.activation(parts[:, :, 1, :], rest[:, :, :], ACT.Copy).then_inc(part1_ready, 1)

            def take_high(i, kind, g):
                if not is_split(kind, g):
                    return
                act.wait_ge(prod_done, number(i, kind, g))
                old = before(i, kind, g, HRING, True)
                if old:
                    act.wait_ge(mm_done, number(*old))
                k, rows = len(tiles(kind, g)), tiles(kind, g)[0][1]
                act.activation(high[0:rows, split_slot(i, kind, g), 0:k, :],
                               prod[0:rows, slot(i, kind, g), 0:k, :], ACT.Copy).then_inc(high_ready, 1)

            def relu0(i):
                act.wait_ge(mm_done, number(i, "L0", G0 - 1))
                if known(i, 1):
                    act.wait_ge(prod_done, number(i - 1, "L1", G1 - 1))
                    act.wait_ge(r01_added, i)
                act.activation(x1[0:HALF, :], z0[0:HALF, :], ACT.Relu,
                               bias=bias_sb[0:HALF, 0:1]).then_inc(x1_ready, 1)
                act.activation(x1[HALF:S, :], z0[0:HALF, :], ACT.Relu,
                               bias=bias_sb[0:HALF, 0:1]).then_inc(x1_ready, 1)
                act.activation(r01[HALF:S, :], z0[HALF:S, :], ACT.Relu,
                               bias=bias_sb[HALF:S, 0:1]).then_inc(r01_ready, 1)

            def relu1(i):
                act.wait_ge(mm_done, number(i, "L1", G1 - 1))
                if known(i, 1):
                    act.wait_ge(prod_done, number(i, "L2", G1 - 1))
                act.activation(x2[0:HALF, :], z1[HALF:S, :], ACT.Relu,
                               bias=bias_sb[HALF:S, 1:2]).then_inc(x2_ready, 1)
                act.activation(x2[HALF:S, :], z1[HALF:S, :], ACT.Relu,
                               bias=bias_sb[HALF:S, 1:2]).then_inc(x2_ready, 1)
                act.activation(r01[0:HALF, :], z1[0:HALF, :], ACT.Relu,
                               bias=bias_sb[0:HALF, 1:2]).then_inc(r01_ready, 1)

            def relu2(i):
                act.wait_ge(mm_done, number(i + 1, "L2", G1 - 1))
                act.activation(r2[:, :], z2[:, :], ACT.Relu, bias=bias_sb[:, 2:3]).then_inc(r2_ready, 1)

            def one_pass(i, first=False, last=False):
                for g in range(G0):
                    take_high(i, "L0", g)
                    if g == 1 and not first:
                        relu1(i - 1)
                if first:
                    relu0(i)
                else:
                    for g in range(G1):
                        take_high(i, "L2", g)
                        if g == 2:
                            relu0(i)
                        if g == 4 and not last:
                            take_part0(i + 1)
                        if g == 6 and not last:
                            take_part1(i + 1)
                for g in range(G1):
                    if first and g == 0:
                        take_part0(i + 1)
                        take_part1(i + 1)
                    take_high(i, "L1", g)
                    if g == 2 and not first:
                        relu2(i - 1)
                    if g == 4 and not last:
                        take_xT(i + 1)
                    if g == 6 and not last:
                        take_base(i + 1)

            act.wait_ge(w0_folded, T0)
            split_weights("L0", w0_sb)
            act.wait_ge(w1_in, 32)
            split_weights("L1", w1_sb)
            act.wait_ge(w2_in, 32)
            split_weights("L2", w2_sb)
            take_part0(0)
            take_part1(0)
            take_xT(0)
            take_base(0)
            act.wait_ge(bias_in, 16)
            one_pass(0, first=True)
            with act.Fori(1, NCH - 1) as i:
                one_pass(i)
            one_pass(NCH - 1, last=True)
            relu1(NCH - 1)
            for g in range(G1):
                take_high(NCH, "L2", g)
            relu2(NCH - 1)

            act.wait_ge(top_in, 16 * 7)
            for m in range(H1 // P):
                act.wait_ge(h1_done, m + 1)
                act.activation(h1[:, m, :], bc[:, m // 2, m % 2, :], ACT.Relu,
                               bias=bt1_sb[:, m:m + 1]).then_inc(h1_ready, 1)
            for m in range(H2 // P):
                act.wait_ge(h2_done, m + 1)
                act.activation(h2[:, m, :], (z0, z1)[m][:, :], ACT.Relu,
                               bias=bt2_sb[:, m:m + 1]).then_inc(h2_ready, 1)
            act.wait_ge(y_done, 1)
            act.activation(y_sb[:, :], z2[0:1, :], ACT.Copy).then_inc(y_ready, 1)

        @block.vector
        def _(dve):
            def take_rest(i):
                dve.wait_ge(part0_ready, i + 1)
                dve.tensor_tensor(rest[:, :, :], x0_of(i), parts[:, :, 0, :], ALU.subtract).then_inc(rest_ready, 1)

            def take_part2(i):
                dve.wait_ge(part1_ready, i + 1)
                dve.tensor_tensor(parts[:, :, 2, :], rest[:, :, :], parts[:, :, 1, :],
                                  ALU.subtract).then_inc(split, 1)

            def free_slot(i, kind, g):
                old = before(i, kind, g, RING)
                if old and is_split(*old[1:]):
                    dve.wait_ge(low_ready, number(*old, True))
                elif old:
                    dve.wait_ge(mm_done, number(*old))

            def take_low(i, kind, g):
                if not is_split(kind, g):
                    return
                dve.wait_ge(high_ready, number(i, kind, g, True))
                old = before(i, kind, g, HRING, True)
                if old:
                    dve.wait_ge(mm_done, number(*old))
                k, rows = len(tiles(kind, g)), tiles(kind, g)[0][1]
                h = split_slot(i, kind, g)
                dve.tensor_tensor(low[0:rows, h, 0:k, :], prod[0:rows, slot(i, kind, g), 0:k, :],
                                  high[0:rows, h, 0:k, :].bitcast(F32), ALU.subtract).then_inc(low_ready, 1)

            def product0(i, g):
                dve.wait_ge(spread_done, i * G0 + g + 1)
                if g == 0:
                    dve.wait_ge(x0_ready, i + 1)
                free_slot(i, "L0", g)
                k, rows = len(tiles("L0", g)), tiles("L0", g)[0][1]
                dve.tensor_tensor(prod[0:rows, slot(i, "L0", g), 0:k, :], bc[0:rows, g % BC, 0:k, :],
                                  x0rep[0:rows, :].unsqueeze(1).to_broadcast([rows, k, N]),
                                  ALU.mult).then_inc(prod_done, 1)

            def product1(i, g):
                if g == 0:
                    dve.wait_ge(x1_ready, 2 * (i + 1))
                if g % PIECE == 0:
                    dve.wait_ge(spread_in[g // PIECE], 32 * (i + 1))
                free_slot(i, "L1", g)
                dve.tensor_tensor(prod[:, slot(i, "L1", g), :, :], spread[:, 2 * g:2 * g + 2, :],
                                  x1[:, :].unsqueeze(1).to_broadcast([P, 2, N]),
                                  ALU.mult).then_inc(prod_done, 1)

            def product2(i, g):
                if g == 0:
                    dve.wait_ge(x2_ready, 2 * (i + 1))
                free_slot(i + 1, "L2", g)
                dve.tensor_tensor(prod[:, slot(i + 1, "L2", g), :, :], spread[:, 2 * g:2 * g + 2, :],
                                  x2[:, :].unsqueeze(1).to_broadcast([P, 2, N]),
                                  ALU.mult).then_inc(prod_done, 1)

            def add01(i):
                dve.wait_ge(r01_ready, 2 * (i + 1))
                a = acc01[:, bass.ds(i // QPB, 1), :].rearrange("p a n -> p (a n)")
                dve.tensor_tensor(a, a, r01[:, :], ALU.add).then_inc(r01_added, 1)

            def add2(i):
                dve.wait_ge(r2_ready, i + 1)
                a = acc2[:, bass.ds(i // QPB, 1), :].rearrange("p a n -> p (a n)")
                dve.tensor_tensor(a, a, r2[:, :], ALU.add).then_inc(r2_added, 1)

            def one_pass(i, first=False, last=False):
                order = FIRST if first else EVERY
                for n, (kind, g) in enumerate(order):
                    if first and (kind, g) == L1S[0]:
                        for x in L0S[-LAG:]:
                            take_low(i, *x)
                    if n >= LAG and not (first and order[n - LAG] in L0S[-LAG:]):
                        take_low(i, *order[n - LAG])
                    if kind == "L0":
                        product0(i, g)
                    elif kind == "L2":
                        product2(i - 1, g)
                    else:
                        product1(i, g)
                    if (kind, g) == ("L2", 1):
                        add01(i - 1)
                    if (kind, g) == (("L1", 0) if first else ("L2", 4)) and not last:
                        take_rest(i + 1)
                    if (kind, g) == (("L1", 1) if first else ("L2", 7)) and not last:
                        take_part2(i + 1)
                    if (kind, g) == ("L1", 6) and not first:
                        add2(i - 1)

            def split_weights(kind, w, done):
                dve.wait_ge(high_w_ready, done)
                for n, g in enumerate(SPLIT[kind]):
                    for j, (t, rows) in enumerate(tiles(kind, g)):
                        last = dve.tensor_tensor(low_w[kind][0:rows, n, j, :], w[0:rows, t, :],
                                                 high_w[kind][0:rows, n, j, :].bitcast(F32), ALU.subtract)
                last.then_inc(low_w_ready, 1)

            dve.memset(acc01[:, :, :], 0.0)
            dve.memset(acc2[:, :, :], 0.0)
            dve.wait_ge(w0_in, 16 * 4)
            for t in range(T0):
                r = R0_LAST if t == T0 - 1 else R0
                dve.tensor_tensor(w0_sb[0:r, t, :], w0_sb[0:r, t, :], w0m_sb[0:r, t, :], ALU.add
                                  ).then_inc(w0_folded, 1)
            split_weights("L0", w0_sb, 1)
            split_weights("L1", w1_sb, 2)
            split_weights("L2", w2_sb, 3)
            take_rest(0)
            take_part2(0)
            one_pass(0, first=True)
            with dve.Fori(1, NCH - 1) as i:
                one_pass(i)
            one_pass(NCH - 1, last=True)
            for g in range(G1 + LAG):
                if g >= LAG:
                    take_low(NCH, "L2", g - LAG)
                if g < G1:
                    product2(NCH - 1, g)
                if g == 1:
                    add01(NCH - 1)
            dve.wait_ge(r01_added, NCH)
            dve.tensor_reduce(logit01.rearrange("p (t b) -> p t b", b=P),
                              acc01[:, :, :].rearrange("p t (d b) -> p t b d", d=DC), AX.X, ALU.add
                              ).then_inc(logits_ready, 1)
            add2(NCH - 1)
            dve.wait_ge(r2_added, NCH)
            dve.tensor_reduce(logit2.rearrange("p (t b) -> p t b", b=P),
                              acc2[:, :, :].rearrange("p t (d b) -> p t b d", d=DC), AX.X, ALU.add
                              ).then_inc(logits_ready, 1)

        @block.tensor
        def _(pe):
            def turn(i):
                pe.wait_ge(split, i + 1)
                if known(i, 1):
                    pe.wait_ge(x0_ready, i)
                for d in range(DC):
                    last = pe.transpose(auxT[0:SR, d * P:(d + 1) * P],
                                        parts[:, d, :, :].rearrange("p a f -> p (a f)"), ident_sb[:, :])
                last.then_inc(transposed, 1)

            def chosen(i, m, rows, dst):
                return pe.matmul(dst, sel_sb[:, m, 0:rows],
                                 xT[:, bass.ds(i % 2, 1), :].rearrange("p a n -> p (a n)"), start=True, stop=True)

            def base(i):
                pe.wait_ge(xT_ready, i + 1)
                chosen(i, 0, R0, aux[0:R0, :]).then_inc(base_done, 1)

            def spread_rows(i, g):
                if g < BC:
                    if known(i, 1):
                        pe.wait_ge(prod_done, number(i - 1, "L0", G0 - BC + g))
                else:
                    pe.wait_ge(prod_done, number(i, "L0", g - BC))
                for j, (t, rows) in enumerate(tiles("L0", g)):
                    last = chosen(i, 1 + t, rows, bc[0:rows, g % BC, j, :])
                last.then_inc(spread_done, 1)

            def sum_group(i, kind, g):
                z, w = {"L0": (z0, w0_sb), "L1": (z1, w1_sb), "L2": (z2, w2_sb)}[kind]
                if g == 0 and known(i, 1):
                    if kind == "L0":
                        pe.wait_ge(r01_ready, 2 * i - 1)
                    elif kind == "L1":
                        pe.wait_ge(r01_ready, 2 * i)
                count = T0 if kind == "L0" else T1
                rows_of = tiles(kind, g)
                if not is_split(kind, g):
                    pe.wait_ge(prod_done, number(i, kind, g))
                    for j, (t, rows) in enumerate(rows_of):
                        last = pe.matmul(z[:, :], w[0:rows, t, :], prod[0:rows, slot(i, kind, g), j, :],
                                         start=(t == 0), stop=(t == count - 1))
                else:
                    n, h = SPLIT[kind].index(g), split_slot(i, kind, g)
                    pe.wait_ge(high_ready, number(i, kind, g, True))
                    for j, (t, rows) in enumerate(rows_of):
                        for v in (high_w, low_w):
                            pe.matmul(z[:, :], v[kind][0:rows, n, j, :], high[0:rows, h, j, :],
                                      start=(t == 0 and v is high_w), stop=False)
                    pe.wait_ge(low_ready, number(i, kind, g, True))
                    for j, (t, rows) in enumerate(rows_of):
                        last = pe.matmul(z[:, :], high_w[kind][0:rows, n, j, :], low[0:rows, h, j, :],
                                         start=False, stop=(t == count - 1))
                last.then_inc(mm_done, 1)

            def one_pass(i, first=False, last=False):
                for g in range(G0):
                    if g + BC < G0:
                        spread_rows(i, g + BC)
                    sum_group(i, "L0", g)
                if not first:
                    for g in range(G1):
                        sum_group(i, "L2", g)
                for g in range(G1):
                    sum_group(i, "L1", g)
                    if last:
                        continue
                    if g == 1:
                        turn(i + 1)
                    if g == 3:
                        base(i + 1)
                    if g in (4, 5):
                        spread_rows(i + 1, g - 4)

            pe.wait_ge(sel_in, 32)
            turn(0)
            base(0)
            for g in range(BC):
                spread_rows(0, g)
            pe.wait_ge(w0_folded, T0)
            pe.wait_ge(low_w_ready, 3)
            one_pass(0, first=True)
            with pe.Fori(1, NCH - 1) as i:
                one_pass(i)
            one_pass(NCH - 1, last=True)
            for g in range(G1):
                sum_group(NCH, "L2", g)

            pe.wait_ge(top_in, 16 * 7)
            pe.wait_ge(logits_ready, 2)
            for m in range(H1 // P):
                o = bc[:, m // 2, m % 2, :]
                cols = slice(m * P, (m + 1) * P)
                pe.matmul(o, wt1c_sb[:, cols], ctx_sb[:, :], start=True, stop=False)
                pe.matmul(o, wt1_sb[:, 0, cols], logit01[:, :], start=False, stop=False)
                pe.matmul(o, wt1_sb[:, 1, cols], logit2[:, :], start=False, stop=True).then_inc(h1_done, 1)
            for m in range(H2 // P):
                for k in range(H1 // P):
                    if m == 0:
                        pe.wait_ge(h1_ready, k + 1)
                    last = pe.matmul((z0, z1)[m][:, :], wt2_sb[:, k, m * P:(m + 1) * P], h1[:, k, :],
                                     start=(k == 0), stop=(k == H1 // P - 1))
                last.then_inc(h2_done, 1)
            for k in range(H2 // P):
                pe.wait_ge(h2_ready, k + 1)
                last = pe.matmul(z2[0:1, :], wt3_sb[:, k:k + 1], h2[:, k, :],
                                 start=(k == 0), stop=(k == H2 // P - 1))
            last.then_inc(y_done, 1)


def selection(bf16):
    take = np.zeros((NSEL, P), np.int64)
    take[0, :] = np.arange(P) % F
    for t in range(T0):
        for j in range(DPT):
            n = t * DPT + j
            if n < len(DELTAS):
                take[1 + t, j * F:(j + 1) * F] = (np.arange(F) + DELTAS[n]) % F
    rows = np.arange(SR) % F
    return (rows[:, None, None] == take[None, :, :]).astype(bf16)


def kernel(**inputs):
    import ml_dtypes
    import concourse.bacc as bacc
    from concourse.bass_utils import run_bass_kernel_spmd

    a = {k: np.asarray(v) for k, v in inputs.items()}
    bf16 = ml_dtypes.bfloat16
    fields = np.arange(F)
    h_of = np.concatenate([fields for _ in DELTAS])
    k_of = np.concatenate([(fields + d) % F for d in DELTAS])
    mirrored = (len(DELTAS) - 1) * F
    swap = np.concatenate([np.arange(HALF, S), np.arange(HALF)])
    wt1 = a["W_top1"]
    arrays = {
        "ids": a["ids"],
        "sel": selection(bf16),
        "ident": np.eye(P).astype(bf16),
        "w0a": a["L0_rec_w0"][h_of, k_of],
        "w0b": a["L0_rec_w0"][k_of, h_of][:mirrored],
        "w1": a["L0_rec_w1"].reshape(F * HALF, S)[:, swap],
        "w2": a["L0_rec_w2"].reshape(F * HALF, S),
        "biases": np.stack([a["L0_rec_b0"], a["L0_rec_b1"][swap], a["L0_rec_b2"]], axis=1),
        "wt1": np.concatenate([wt1[HALF:S], wt1[:HALF], wt1[S:]], axis=0),
        "bt1": a["b_top1"].reshape(-1, P).T,
        "wt2": a["W_top2"],
        "bt2": a["b_top2"].reshape(-1, P).T,
        "wt3": a["W_top3"].reshape(-1, P).T,
        "ctxT": a["dense_ctx"].T,
    }
    for f in range(F):
        arrays[f"tbl_{f}"] = a[f"tbl_{f}"]
    arrays = {f"{k}_dram": np.ascontiguousarray(v) for k, v in arrays.items()}
    nc = bacc.Bacc("TRN2", target_bir_lowering=False, num_devices=1)
    ap = {k: nc.dram_tensor(k, v.shape, mybir.dt.from_np(v.dtype), kind="ExternalInput").ap()
          for k, v in arrays.items()}
    out = nc.dram_tensor("out_dram", (B, 1), F32, kind="ExternalOutput").ap()
    tower_kernel(nc, ap["ids_dram"], [ap[f"tbl_{f}_dram"] for f in range(F)],
                 *[ap[f"{k}_dram"] for k in ("sel", "ident", "w0a", "w0b", "w1", "w2", "biases",
                                             "wt1", "bt1", "wt2", "bt2", "wt3", "ctxT")], out)
    r = run_bass_kernel_spmd(nc, [arrays], core_ids=[0])
    return r.results[0]["out_dram"]
```

```python
from contextlib import ExitStack

import numpy as np

import concourse.bass as bass
from concourse import mybir

P = 128
B = 512
F = 39
D = 16
S = 128
HALF = S // 2
DENSE = 16
H1, H2 = 512, 256
NBT = B // P
DC = 4
QPB = D // DC
N = DC * P
NCH = NBT * QPB
PARTS = 3
SR = PARTS * F

DELTAS = list(range((F + 1) // 2))
DPT = P // F
T0 = -(-len(DELTAS) // DPT)
R0 = DPT * F
R0_LAST = (len(DELTAS) - (T0 - 1) * DPT) * F
T1 = -(-F // 2)
R1_LAST = (F - (T1 - 1) * 2) * HALF
G0 = T0 // 2 + T0 % 2
G1 = T1 // 2

RING = 8
HRING = 3
LAG = 2

L0S = [("L0", g) for g in range(G0)]
L1S = [("L1", g) for g in range(G1)]
L2S = [("L2", g) for g in range(G1)]
FIRST, EVERY = L0S + L1S, L0S + L2S + L1S
PIECE = 2
PIECES = G1 // PIECE

DVE_LOW = {"L0": (1,), "L2": (1, 7), "L1": (0, 3, 6)}
POOL_LOW = {"L0": (), "L2": (3, 5, 8), "L1": (1, 4, 7)}
ADD01_AT, ADD2_AT = ("L2", 0), ("L1", 8)
SPLIT = {k: tuple(sorted(DVE_LOW[k] + POOL_LOW[k])) for k in POOL_LOW}

GATHERS = {1: range(0, 3), 2: range(3, 7), 3: range(7, 11)}

ALU = mybir.AluOpType
ACT = mybir.ActivationFunctionType
AX = mybir.AxisListType
F32 = mybir.dt.float32
F32R = mybir.dt.float32r
BF16 = mybir.dt.bfloat16
I32 = mybir.dt.int32


def known(i, least):
    return not isinstance(i, int) or i >= least


def all_of(i):
    return FIRST if isinstance(i, int) and i == 0 else L2S if isinstance(i, int) and i == NCH else EVERY


def among(groups, which):
    return [(k, g) for k, g in groups if which is None or g in which[k]]


def number(i, kind, g, which=None):
    at = among(all_of(i), which).index((kind, g)) + 1
    if isinstance(i, int) and i == 0:
        return at
    return (i - 1) * len(among(EVERY, which)) + len(among(FIRST, which)) + at


def before(i, kind, g, back, which=None):
    order = among(all_of(i), which)
    at = order.index((kind, g)) - back
    if at >= 0:
        return (i, *order[at])
    if not known(i, 1):
        return None
    assert among(FIRST, which)[at] == among(EVERY, which)[at]
    return (i - 1, *among(EVERY, which)[at])


def slot(i, kind, g):
    return (number(i if isinstance(i, int) else 1, kind, g) - 1) % RING


def split_slot(i, kind, g):
    return (number(i if isinstance(i, int) else 1, kind, g, SPLIT) - 1) % HRING


assert len(EVERY) % RING == 0 and T1 % 2 == 0 and G1 % PIECE == 0
assert len(among(EVERY, SPLIT)) % HRING == 0
assert not among(EVERY[-LAG:], DVE_LOW)


def tiles(kind, g):
    out = []
    last, full, end = (T0, R0, R0_LAST) if kind == "L0" else (T1, P, R1_LAST)
    for t in (2 * g, 2 * g + 1):
        if t < last:
            out.append((t, end if t == last - 1 else full))
    return out


def tower_kernel(nc, ids, tbls, sel, ident, w0a, w0b, w1, w2, biases, wt1, bt1, wt2, bt2, wt3, ctxT, out):
    with ExitStack() as ctx:
        def sb(name, shape, dt=F32):
            return ctx.enter_context(nc.sbuf_tensor(name, shape, dt))

        def psum(name, shape, dt=F32):
            return ctx.enter_context(nc.psum_tensor(name, shape, dt))

        def sem(name):
            return ctx.enter_context(nc.semaphore(name))

        ids_sb = sb("ids_sb", [P, NBT, F], I32)
        emb = sb("emb", [P, NBT, F, D])
        sel_sb = sb("sel_sb", [SR, 1 + T0, P], BF16)
        ident_sb = sb("ident_sb", [P, P], BF16)
        w0_sb = sb("w0_sb", [R0, T0, S])
        w1_sb = sb("w1_sb", [P, T1, S])
        w2_sb = sb("w2_sb", [P, T1, S])
        high_w = {k: sb(f"high_w_{k}", [P, len(SPLIT[k]), 2, S], F32R) for k in SPLIT}
        low_w = {k: sb(f"low_w_{k}", [P, len(SPLIT[k]), 2, S], F32R) for k in SPLIT}
        bias_sb = sb("bias_sb", [S, 3])
        rest = sb("rest", [P, DC, F])
        parts = sb("parts", [P, DC, PARTS, F], BF16)
        xT = sb("xT", [SR, N], BF16)
        x0rows = sb("x0rows", [R0, N])
        spread0 = sb("spread0", [P, 2 * G0, N])
        spread = sb("spread", [P, T1, N])
        x0_dram = nc.dram_tensor("x0_rows", [NCH, 2 * F, N], F32, kind="Internal")
        prod = sb("prod", [P, RING, 2, N])
        w0m_sb = prod[0:R0, 0, :, :].rearrange("p a n -> p (a n)")[:, 0:T0 * S].rearrange("p (t s) -> p t s", s=S)
        high = sb("high", [P, HRING, 2, N], F32R)
        low = sb("low", [P, HRING, 2, N], F32R)
        r01 = sb("r01", [P, N])
        r2 = sb("r2", [P, N])
        fold = sb("fold", [P, 2, N // 2])
        logit01 = sb("logit01", [P, B])
        logit2 = sb("logit2", [P, B])
        ctx_sb = sb("ctx_sb", [DENSE, B])
        wt1_sb = sb("wt1_sb", [P, 2, H1])
        wt1c_sb = sb("wt1c_sb", [DENSE, H1])
        bt1_sb = sb("bt1_sb", [P, H1 // P])
        wt2_sb = sb("wt2_sb", [P, H1 // P, H2])
        bt2_sb = sb("bt2_sb", [P, H2 // P])
        wt3_sb = sb("wt3_sb", [P, H2 // P])
        y_sb = sb("y_sb", [1, B])
        h1 = spread[:, 0:H1 // P, :]
        h2 = spread[:, H1 // P:H1 // P + H2 // P, :]

        base = psum("base", [P, N])
        x12 = psum("x12", [P, 2, N])
        x1, x2 = x12[:, 0, :], x12[:, 1, :]
        z0 = psum("z0", [P, N])
        z12 = psum("z12", [P, 2, N])
        z1, z2 = z12[:, 0, :], z12[:, 1, :]
        turned = psum("turned", [P, N], BF16)
        spare = psum("spare", [P, N])
        h1_sum, h2_sum = (z0, x1, base, spare), (z1, x2)

        def x0_of(i):
            return emb[:, bass.ds(i // QPB, 1), :, bass.ds((i % QPB) * DC, DC)].rearrange("p a f d -> p (a d) f")

        ids_in = sem("ids_in")
        sel_in = sem("sel_in")
        w0_in = sem("w0_in")
        w1_in = sem("w1_in")
        w2_in = sem("w2_in")
        bias_in = sem("bias_in")
        top_in = sem("top_in")
        tile_in = [sem(f"tile_in{t}") for t in range(NBT)]
        gathered = sem("gathered")
        zeroed = sem("zeroed")
        edge_zeroed = sem("edge_zeroed")
        w0_folded = sem("w0_folded")
        high_w_ready = sem("high_w_ready")
        low_w_ready = sem("low_w_ready")
        part0_ready = sem("part0_ready")
        rest_ready = sem("rest_ready")
        part1_ready = sem("part1_ready")
        split = sem("split")
        transposed = sem("transposed")
        xT_ready = sem("xT_ready")
        base_done = sem("base_done")
        x0_ready = sem("x0_ready")
        x0_stored = sem("x0_stored")
        spread_in = [sem(f"spread_in{p}") for p in range(PIECES)]
        first_spread = sem("first_spread")
        spread0_in = sem("spread0_in")
        prod_done = sem("prod_done")
        high_ready = sem("high_ready")
        dve_low = sem("dve_low")
        pool_low = sem("pool_low")
        mm_done = sem("mm_done")
        x1_ready = sem("x1_ready")
        x2_ready = sem("x2_ready")
        r01_ready = sem("r01_ready")
        r2_ready = sem("r2_ready")
        folded = sem("folded")
        r01_free = sem("r01_free")
        r2_free = sem("r2_free")
        h1_done = sem("h1_done")
        h1_ready = sem("h1_ready")
        h2_done = sem("h2_done")
        h2_ready = sem("h2_ready")
        y_done = sem("y_done")
        y_ready = sem("y_ready")
        out_written = sem("out_written")

        block = ctx.enter_context(nc.Block())

        @block.sync
        def _(sp):
            sp.dma_start(ids_sb[:, :, :], ids.rearrange("(t p) f -> p t f", p=P)).then_inc(ids_in, 16)
            sp.dma_start(sel_sb[:, :, :], sel).then_inc(sel_in, 16)
            sp.dma_start(ident_sb[:, :], ident).then_inc(sel_in, 16)
            full0 = (T0 - 1) * R0
            sp.wait_ge(zeroed, 1)
            sp.dma_start(w0_sb[:, 0:T0 - 1, :],
                         w0a[0:full0, :].rearrange("(t p) s -> p t s", p=R0)).then_inc(w0_in, 16)
            sp.dma_start(w0_sb[0:R0_LAST, T0 - 1, :], w0a[full0:, :]).then_inc(w0_in, 16)
            sp.dma_start(w0m_sb[F:R0, 0, :], w0b[0:R0 - F, :]).then_inc(w0_in, 16)
            sp.dma_start(w0m_sb[:, 1:T0 - 1, :],
                         w0b[R0 - F:full0 - F, :].rearrange("(t p) s -> p t s", p=R0)).then_inc(w0_in, 16)
            sp.dma_start(w0m_sb[0:R0_LAST, T0 - 1, :], w0b[full0 - F:, :]).then_inc(w0_in, 16)
            sp.dma_start(bias_sb[:, :], biases).then_inc(bias_in, 16)
            full1 = (T1 - 1) * P
            for w, w_sb, s in ((w1, w1_sb, w1_in), (w2, w2_sb, w2_in)):
                sp.dma_start(w_sb[:, 0:T1 - 1, :],
                             w[0:full1, :].rearrange("(t p) s -> p t s", p=P)).then_inc(s, 16)
                sp.dma_start(w_sb[0:R1_LAST, T1 - 1, :], w[full1:, :]).then_inc(s, 16)
            sp.dma_start(wt1_sb[:, :, :], wt1[0:2 * P, :].rearrange("(t p) n -> p t n", p=P)).then_inc(top_in, 16)
            sp.dma_start(wt1c_sb[:, :], wt1[2 * P:, :]).then_inc(top_in, 16)
            sp.dma_start(bt1_sb[:, :], bt1).then_inc(top_in, 16)
            sp.dma_start(wt2_sb[:, :, :], wt2.rearrange("(t p) n -> p t n", p=P)).then_inc(top_in, 16)
            sp.dma_start(bt2_sb[:, :], bt2).then_inc(top_in, 16)
            sp.dma_start(wt3_sb[:, :], wt3).then_inc(top_in, 16)
            sp.dma_start(ctx_sb[:, :], ctxT).then_inc(top_in, 16)

            def store_x0(i):
                sp.wait_ge(x0_ready, i + 1)
                sp.dma_start(x0_dram[bass.ds(i, 1), :, :].rearrange("a f n -> (a f) n"),
                             x0rows[0:2 * F, :]).then_inc(x0_stored, 16)
                sp.wait_ge(x0_stored, 16 * (i + 1))
                if not known(i, 1):
                    return
                for j in range(DPT):
                    many = len(range(j, len(DELTAS), DPT))
                    row = x0_dram[bass.ds(i, 1), j:j + F, :]
                    src = bass.AP(row.tensor, row.offset, [[N, F], [DPT * N, many], [1, N]])
                    sp.dma_start(spread0[j * F:(j + 1) * F, 0:many, :], src).then_inc(spread0_in, 16)

            def spread_piece(i, p):
                if known(i, 1):
                    sp.wait_ge(prod_done, number(i, "L2", PIECE * (p + 1) - 1))
                for half in range(2):
                    t = 2 * PIECE * p
                    many = len(range(2 * t + half, min(F, 2 * t + 4 * PIECE), 2))
                    src = x0_dram[bass.ds(i, 1), bass.ds(2 * t + half, many, 2), :].rearrange("a f n -> (a f) n")
                    sp.dma_start(spread[half * HALF:(half + 1) * HALF, t:t + many, :],
                                 src.unsqueeze(0).to_broadcast([HALF, many, N])).then_inc(spread_in[p], 16)

            store_x0(0)
            sp.wait_ge(edge_zeroed, 1)
            for p in range(PIECES):
                spread_piece(0, p)
            store_x0(1)
            with sp.Fori(1, NCH - 1) as i:
                for p in range(PIECES):
                    spread_piece(i, p)
                store_x0(i + 1)
            for p in range(PIECES):
                spread_piece(NCH - 1, p)

            sp.wait_ge(y_ready, 1)
            sp.dma_start(out.rearrange("b o -> o b"), y_sb[:, :]).then_inc(out_written, 16)
            sp.wait_ge(out_written, 16)

        @block.gpsimd
        def _(pool):
            pool.memset(w0m_sb[:, 0, :], 0.0).then_inc(zeroed, 1)
            pool.wait_ge(zeroed, 1)
            pool.memset(spread[HALF:P, T1 - 1, :], 0.0).then_inc(edge_zeroed, 1)
            pool.wait_ge(edge_zeroed, 1)
            pool.wait_ge(ids_in, 16)

            def gather(t, f):
                pool.indirect_dma_start(
                    out=emb[:, t, f, :], out_offset=None, in_=tbls[f],
                    in_offset=bass.IndirectOffsetOnAxis(ap=ids_sb[:, t, f:f + 1], axis=0),
                ).then_inc(tile_in[t], 16)

            def tell_gathered(t):
                pool.wait_ge(tile_in[t], 16 * F)
                pool.sem_inc(gathered, 1)

            def take_low(i, kind, g):
                if g not in POOL_LOW[kind]:
                    return
                pool.wait_ge(high_ready, number(i, kind, g, SPLIT))
                old = before(i, kind, g, HRING, SPLIT)
                if old:
                    pool.wait_ge(mm_done, number(*old))
                k, rows = len(tiles(kind, g)), tiles(kind, g)[0][1]
                h = split_slot(i, kind, g)
                pool.tensor_tensor(low[0:rows, h, 0:k, :], prod[0:rows, slot(i, kind, g), 0:k, :],
                                   high[0:rows, h, 0:k, :].bitcast(F32), ALU.subtract).then_inc(pool_low, 1)

            def add(i, r, logit, which, free):
                half, sample = N // 2, logit[:, bass.ds((i // QPB) * P, P)]
                pool.tensor_tensor(fold[:, which, :], r[:, 0:half], r[:, half:N], ALU.add).then_inc(folded, 1)
                pool.wait_ge(folded, 4 * i + 2 * which + 1)
                pool.tensor_tensor(fold[:, which, 0:P], fold[:, which, 0:P], fold[:, which, P:half], ALU.add).then_inc(folded, 1)
                pool.wait_ge(folded, 4 * i + 2 * which + 2)
                pool.tensor_tensor(sample, sample, fold[:, which, 0:P], ALU.add).then_inc(free, 1)

            def add01(i):
                pool.wait_ge(r01_ready, 2 * (i + 1))
                add(i, r01, logit01, 0, r01_free)

            def add2(i):
                pool.wait_ge(r2_ready, i + 1)
                add(i, r2, logit2, 1, r2_free)

            def one_pass(i, first=False):
                share = [t for t in GATHERS if isinstance(i, int) and i in GATHERS[t]]
                todo = []
                for t in share:
                    n, m = i - GATHERS[t][0], len(GATHERS[t])
                    todo = [(t, f) for f in range(F * n // m, F * (n + 1) // m)]
                for t in GATHERS:
                    if isinstance(i, int) and i == GATHERS[t][-1] + 1:
                        tell_gathered(t)
                idle = [x for x in all_of(i) if x[1] not in POOL_LOW[x[0]] and x not in (ADD01_AT, ADD2_AT)]
                for kind, g in all_of(i):
                    take_low(i, kind, g)
                    if (kind, g) in idle:
                        many = -(-len(todo) // (len(idle) - idle.index((kind, g))))
                        for _ in range(many):
                            gather(*todo.pop(0))
                    if (kind, g) == ADD01_AT and not first:
                        add01(i - 1)
                    if (kind, g) == ADD2_AT and not first:
                        add2(i - 1)
                assert not todo

            pool.memset(logit01[:, :], 0.0).then_inc(r01_free, 1)
            pool.memset(logit2[:, :], 0.0).then_inc(r2_free, 1)
            for f in range(F):
                gather(0, f)
            tell_gathered(0)
            one_pass(0, first=True)
            ends = GATHERS[NBT - 1][-1] + 2
            for i in range(1, ends):
                one_pass(i)
            with pool.Fori(ends, NCH) as i:
                one_pass(i)
            for g in range(G1):
                take_low(NCH, "L2", g)
            add01(NCH - 1)
            add2(NCH - 1)

        @block.scalar
        def _(act):
            def split_weights(kind, w):
                for n, g in enumerate(SPLIT[kind]):
                    for j, (t, rows) in enumerate(tiles(kind, g)):
                        last = act.activation(high_w[kind][0:rows, n, j, :], w[0:rows, t, :], ACT.Copy)
                last.then_inc(high_w_ready, 1)

            def take_xT(i):
                act.wait_ge(transposed, i + 1)
                act.activation(xT[:, :], turned[0:SR, :], ACT.Copy).then_inc(xT_ready, 1)

            def take_rows(i):
                act.wait_ge(base_done, i + 1)
                if known(i, 1):
                    act.wait_ge(x0_stored, 16 * i)
                act.activation(x0rows[:, :], base[0:R0, :], ACT.Copy).then_inc(x0_ready, 1)

            def take_part0(i):
                act.wait_ge(gathered, (i // QPB) + 1)
                if known(i, 1):
                    act.wait_ge(transposed, i)
                act.activation(parts[:, :, 0, :], x0_of(i), ACT.Copy).then_inc(part0_ready, 1)

            def take_part1(i):
                act.wait_ge(rest_ready, i + 1)
                act.activation(parts[:, :, 1, :], rest[:, :, :], ACT.Copy).then_inc(part1_ready, 1)

            def take_high(i, kind, g):
                if g not in SPLIT[kind]:
                    return
                act.wait_ge(prod_done, number(i, kind, g))
                old = before(i, kind, g, HRING, SPLIT)
                if old:
                    act.wait_ge(mm_done, number(*old))
                k, rows = len(tiles(kind, g)), tiles(kind, g)[0][1]
                act.activation(high[0:rows, split_slot(i, kind, g), 0:k, :],
                               prod[0:rows, slot(i, kind, g), 0:k, :], ACT.Copy).then_inc(high_ready, 1)

            def relu0(i):
                act.wait_ge(mm_done, number(i, "L0", G0 - 1))
                if known(i, 1):
                    act.wait_ge(prod_done, number(i - 1, "L1", G1 - 1))
                    act.wait_ge(r01_free, i + 1)
                act.activation(x1[0:HALF, :], z0[0:HALF, :], ACT.Relu,
                               bias=bias_sb[0:HALF, 0:1]).then_inc(x1_ready, 1)
                act.activation(x1[HALF:S, :], z0[0:HALF, :], ACT.Relu,
                               bias=bias_sb[0:HALF, 0:1]).then_inc(x1_ready, 1)
                act.activation(r01[HALF:S, :], z0[HALF:S, :], ACT.Relu,
                               bias=bias_sb[HALF:S, 0:1]).then_inc(r01_ready, 1)

            def relu1(i):
                act.wait_ge(mm_done, number(i, "L1", G1 - 1))
                if known(i, 1):
                    act.wait_ge(prod_done, number(i, "L2", G1 - 1))
                act.activation(x2[0:HALF, :], z1[HALF:S, :], ACT.Relu,
                               bias=bias_sb[HALF:S, 1:2]).then_inc(x2_ready, 1)
                act.activation(x2[HALF:S, :], z1[HALF:S, :], ACT.Relu,
                               bias=bias_sb[HALF:S, 1:2]).then_inc(x2_ready, 1)
                act.activation(r01[0:HALF, :], z1[0:HALF, :], ACT.Relu,
                               bias=bias_sb[0:HALF, 1:2]).then_inc(r01_ready, 1)

            def relu2(i):
                act.wait_ge(mm_done, number(i + 1, "L2", G1 - 1))
                act.wait_ge(r2_free, i + 1)
                act.activation(r2[:, :], z2[:, :], ACT.Relu, bias=bias_sb[:, 2:3]).then_inc(r2_ready, 1)

            def one_pass(i, first=False, last=False):
                for g in range(G0):
                    take_high(i, "L0", g)
                if not first:
                    relu1(i - 1)
                if first:
                    act.wait_ge(first_spread, G0)
                    take_xT(i + 1)
                    relu0(i)
                    take_rows(i + 1)
                else:
                    for g in range(G1):
                        take_high(i, "L2", g)
                        if g == 2:
                            relu0(i)
                        if last:
                            continue
                        if g == 0:
                            take_part0(i + 1)
                        if g == 3:
                            take_part1(i + 1)
                        if g == 6:
                            take_xT(i + 1)
                        if g == 9:
                            take_rows(i + 1)
                for g in range(G1):
                    take_high(i, "L1", g)
                    if not first and g == 2:
                        relu2(i - 1)

            act.wait_ge(w0_folded, T0)
            split_weights("L0", w0_sb)
            act.wait_ge(w1_in, 32)
            split_weights("L1", w1_sb)
            act.wait_ge(w2_in, 32)
            split_weights("L2", w2_sb)
            take_part0(0)
            take_part1(0)
            take_xT(0)
            take_part0(1)
            take_rows(0)
            take_part1(1)
            act.wait_ge(bias_in, 16)
            one_pass(0, first=True)
            with act.Fori(1, NCH - 1) as i:
                one_pass(i)
            one_pass(NCH - 1, last=True)
            relu1(NCH - 1)
            for g in range(G1):
                take_high(NCH, "L2", g)
            relu2(NCH - 1)

            act.wait_ge(top_in, 16 * 7)
            for m in range(H1 // P):
                act.wait_ge(h1_done, m + 1)
                act.activation(h1[:, m, :], h1_sum[m][:, :], ACT.Relu,
                               bias=bt1_sb[:, m:m + 1]).then_inc(h1_ready, 1)
            for m in range(H2 // P):
                act.wait_ge(h2_done, m + 1)
                act.activation(h2[:, m, :], h2_sum[m][:, :], ACT.Relu,
                               bias=bt2_sb[:, m:m + 1]).then_inc(h2_ready, 1)
            act.wait_ge(y_done, 1)
            act.activation(y_sb[:, :], z0[0:1, :], ACT.Copy).then_inc(y_ready, 1)

        @block.vector
        def _(dve):
            def take_rest(i):
                dve.wait_ge(part0_ready, i + 1)
                dve.tensor_tensor(rest[:, :, :], x0_of(i), parts[:, :, 0, :], ALU.subtract).then_inc(rest_ready, 1)

            def take_part2(i):
                dve.wait_ge(part1_ready, i + 1)
                dve.tensor_tensor(parts[:, :, 2, :], rest[:, :, :], parts[:, :, 1, :],
                                  ALU.subtract).then_inc(split, 1)

            def free_slot(i, kind, g):
                old = before(i, kind, g, RING)
                if old:
                    _, k, at = old
                    if at in DVE_LOW[k]:
                        dve.wait_ge(dve_low, number(*old, DVE_LOW))
                    elif at in POOL_LOW[k]:
                        dve.wait_ge(pool_low, number(*old, POOL_LOW))
                    else:
                        dve.wait_ge(mm_done, number(*old))

            def take_low(i, kind, g):
                if g not in DVE_LOW[kind]:
                    return
                dve.wait_ge(high_ready, number(i, kind, g, SPLIT))
                old = before(i, kind, g, HRING, SPLIT)
                if old:
                    dve.wait_ge(mm_done, number(*old))
                k, rows = len(tiles(kind, g)), tiles(kind, g)[0][1]
                h = split_slot(i, kind, g)
                dve.tensor_tensor(low[0:rows, h, 0:k, :], prod[0:rows, slot(i, kind, g), 0:k, :],
                                  high[0:rows, h, 0:k, :].bitcast(F32), ALU.subtract).then_inc(dve_low, 1)

            def product0(i, g):
                if g == 0:
                    dve.wait_ge(x0_ready, i + 1)
                    if known(i, 1):
                        dve.wait_ge(spread0_in, 16 * DPT * i)
                free_slot(i, "L0", g)
                k, rows = len(tiles("L0", g)), tiles("L0", g)[0][1]
                if known(i, 1):
                    factors, shared = spread0[0:rows, 2 * g:2 * g + k, :], base
                else:
                    dve.wait_ge(first_spread, g + 1)
                    factors, shared = (z12, x12)[g % 2][0:rows, 0:k, :], x0rows
                dve.tensor_tensor(prod[0:rows, slot(i, "L0", g), 0:k, :], factors,
                                  shared[0:rows, :].unsqueeze(1).to_broadcast([rows, k, N]),
                                  ALU.mult).then_inc(prod_done, 1)

            def product1(i, g):
                if g == 0:
                    dve.wait_ge(x1_ready, 2 * (i + 1))
                if g % PIECE == 0:
                    dve.wait_ge(spread_in[g // PIECE], 32 * (i + 1))
                free_slot(i, "L1", g)
                dve.tensor_tensor(prod[:, slot(i, "L1", g), :, :], spread[:, 2 * g:2 * g + 2, :],
                                  x1[:, :].unsqueeze(1).to_broadcast([P, 2, N]),
                                  ALU.mult).then_inc(prod_done, 1)

            def product2(i, g):
                if g == 0:
                    dve.wait_ge(x2_ready, 2 * (i + 1))
                free_slot(i + 1, "L2", g)
                dve.tensor_tensor(prod[:, slot(i + 1, "L2", g), :, :], spread[:, 2 * g:2 * g + 2, :],
                                  x2[:, :].unsqueeze(1).to_broadcast([P, 2, N]),
                                  ALU.mult).then_inc(prod_done, 1)

            def one_pass(i, first=False, last=False):
                order = FIRST if first else EVERY
                for n, (kind, g) in enumerate(order):
                    if first and (kind, g) == L1S[0]:
                        for x in L0S[-LAG:]:
                            take_low(i, *x)
                    if n >= LAG and not (first and order[n - LAG] in L0S[-LAG:]):
                        take_low(i, *order[n - LAG])
                    if kind == "L0":
                        product0(i, g)
                    elif kind == "L2":
                        product2(i - 1, g)
                    else:
                        product1(i, g)
                    if (kind, g) == ("L2", 1) and not last:
                        take_rest(i + 1)
                    if (kind, g) == ("L2", 4) and not last:
                        take_part2(i + 1)

            def split_weights(kind, w, done):
                dve.wait_ge(high_w_ready, done)
                for n, g in enumerate(SPLIT[kind]):
                    for j, (t, rows) in enumerate(tiles(kind, g)):
                        last = dve.tensor_tensor(low_w[kind][0:rows, n, j, :], w[0:rows, t, :],
                                                 high_w[kind][0:rows, n, j, :].bitcast(F32), ALU.subtract)
                last.then_inc(low_w_ready, 1)

            dve.wait_ge(w0_in, 16 * 5)
            for t in range(T0):
                r = R0_LAST if t == T0 - 1 else R0
                dve.tensor_tensor(w0_sb[0:r, t, :], w0_sb[0:r, t, :], w0m_sb[0:r, t, :], ALU.add
                                  ).then_inc(w0_folded, 1)
            split_weights("L0", w0_sb, 1)
            split_weights("L1", w1_sb, 2)
            split_weights("L2", w2_sb, 3)
            for i in range(2):
                take_rest(i)
                take_part2(i)
            one_pass(0, first=True)
            with dve.Fori(1, NCH - 1) as i:
                one_pass(i)
            one_pass(NCH - 1, last=True)
            for g in range(G1 + LAG):
                if g >= LAG:
                    take_low(NCH, "L2", g - LAG)
                if g < G1:
                    product2(NCH - 1, g)

        @block.tensor
        def _(pe):
            def turn(i):
                pe.wait_ge(split, i + 1)
                if known(i, 1):
                    pe.wait_ge(xT_ready, i)
                for d in range(DC):
                    last = pe.transpose(turned[0:SR, d * P:(d + 1) * P],
                                        parts[:, d, :, :].rearrange("p a f -> p (a f)"), ident_sb[:, :])
                last.then_inc(transposed, 1)

            def make_base(i):
                pe.wait_ge(xT_ready, i + 1)
                if known(i, 1):
                    pe.wait_ge(x0_ready, i)
                    pe.wait_ge(prod_done, number(i - 1, "L0", G0 - 1))
                pe.matmul(base[0:R0, :], sel_sb[:, 0, 0:R0], xT[:, :], start=True, stop=True).then_inc(base_done, 1)

            def spread_first(g):
                if g >= 2:
                    pe.wait_ge(prod_done, number(0, "L0", g - 2))
                for j, (t, rows) in enumerate(tiles("L0", g)):
                    last = pe.matmul((z12, x12)[g % 2][0:rows, j, :], sel_sb[:, 1 + t, 0:rows], xT[:, :],
                                     start=True, stop=True)
                last.then_inc(first_spread, 1)

            def sum_group(i, kind, g):
                z, w = {"L0": (z0, w0_sb), "L1": (z1, w1_sb), "L2": (z2, w2_sb)}[kind]
                if g == 0 and known(i, 1):
                    if kind == "L0":
                        pe.wait_ge(r01_ready, 2 * i - 1)
                    elif kind == "L1":
                        pe.wait_ge(r01_ready, 2 * i)
                count = T0 if kind == "L0" else T1
                rows_of = tiles(kind, g)
                if g not in SPLIT[kind]:
                    pe.wait_ge(prod_done, number(i, kind, g))
                    for j, (t, rows) in enumerate(rows_of):
                        last = pe.matmul(z[:, :], w[0:rows, t, :], prod[0:rows, slot(i, kind, g), j, :],
                                         start=(t == 0), stop=(t == count - 1))
                else:
                    n, h = SPLIT[kind].index(g), split_slot(i, kind, g)
                    pe.wait_ge(high_ready, number(i, kind, g, SPLIT))
                    for j, (t, rows) in enumerate(rows_of):
                        for v in (high_w, low_w):
                            pe.matmul(z[:, :], v[kind][0:rows, n, j, :], high[0:rows, h, j, :],
                                      start=(t == 0 and v is high_w), stop=False)
                    if g in DVE_LOW[kind]:
                        pe.wait_ge(dve_low, number(i, kind, g, DVE_LOW))
                    else:
                        pe.wait_ge(pool_low, number(i, kind, g, POOL_LOW))
                    for j, (t, rows) in enumerate(rows_of):
                        last = pe.matmul(z[:, :], high_w[kind][0:rows, n, j, :], low[0:rows, h, j, :],
                                         start=False, stop=(t == count - 1))
                last.then_inc(mm_done, 1)

            def one_pass(i, first=False, last=False):
                for g in range(G0):
                    if first and g + 2 < G0:
                        spread_first(g + 2)
                    sum_group(i, "L0", g)
                if first:
                    make_base(i + 1)
                else:
                    for g in range(G1):
                        sum_group(i, "L2", g)
                        if g == 3 and not last:
                            turn(i + 1)
                        if g == 6 and not last:
                            make_base(i + 1)
                for g in range(G1):
                    sum_group(i, "L1", g)

            pe.wait_ge(sel_in, 32)
            turn(0)
            make_base(0)
            for g in range(2):
                spread_first(g)
            turn(1)
            pe.wait_ge(w0_folded, T0)
            pe.wait_ge(low_w_ready, 3)
            one_pass(0, first=True)
            with pe.Fori(1, NCH - 1) as i:
                one_pass(i)
            one_pass(NCH - 1, last=True)
            pe.wait_ge(top_in, 16 * 7)
            pe.wait_ge(r01_ready, 2 * NCH - 1)
            for m in range(H1 // P):
                pe.matmul(h1_sum[m][:, :], wt1c_sb[:, m * P:(m + 1) * P], ctx_sb[:, :], start=True, stop=False)
            for g in range(G1):
                sum_group(NCH, "L2", g)
            pe.wait_ge(r01_free, NCH + 1)
            for m in range(H1 // P):
                pe.matmul(h1_sum[m][:, :], wt1_sb[:, 0, m * P:(m + 1) * P], logit01[:, :], start=False, stop=False)
            pe.wait_ge(r2_free, NCH + 1)
            for m in range(H1 // P):
                pe.matmul(h1_sum[m][:, :], wt1_sb[:, 1, m * P:(m + 1) * P], logit2[:, :],
                          start=False, stop=True).then_inc(h1_done, 1)
            for m in range(H2 // P):
                for k in range(H1 // P):
                    if m == 0:
                        pe.wait_ge(h1_ready, k + 1)
                    last = pe.matmul(h2_sum[m][:, :], wt2_sb[:, k, m * P:(m + 1) * P], h1[:, k, :],
                                     start=(k == 0), stop=(k == H1 // P - 1))
                last.then_inc(h2_done, 1)
            for k in range(H2 // P):
                pe.wait_ge(h2_ready, k + 1)
                last = pe.matmul(z0[0:1, :], wt3_sb[:, k:k + 1], h2[:, k, :],
                                 start=(k == 0), stop=(k == H2 // P - 1))
            last.then_inc(y_done, 1)


def selection(bf16):
    take = np.zeros((1 + T0, P), np.int64)
    take[0, :] = np.arange(P) % F
    for t in range(T0):
        for j in range(DPT):
            n = t * DPT + j
            if n < len(DELTAS):
                take[1 + t, j * F:(j + 1) * F] = (np.arange(F) + DELTAS[n]) % F
    rows = np.arange(SR) % F
    return (rows[:, None, None] == take[None, :, :]).astype(bf16)


def kernel(**inputs):
    import ml_dtypes
    import concourse.bacc as bacc
    from concourse.bass_utils import run_bass_kernel_spmd

    a = {k: np.asarray(v) for k, v in inputs.items()}
    bf16 = ml_dtypes.bfloat16
    fields = np.arange(F)
    h_of = np.concatenate([fields for _ in DELTAS])
    k_of = np.concatenate([(fields + d) % F for d in DELTAS])
    swap = np.concatenate([np.arange(HALF, S), np.arange(HALF)])
    wt1 = a["W_top1"]
    arrays = {
        "ids": a["ids"],
        "sel": selection(bf16),
        "ident": np.eye(P).astype(bf16),
        "w0a": a["L0_rec_w0"][h_of, k_of],
        "w0b": a["L0_rec_w0"][k_of, h_of][F:],
        "w1": a["L0_rec_w1"].reshape(F * HALF, S)[:, swap],
        "w2": a["L0_rec_w2"].reshape(F * HALF, S),
        "biases": np.stack([a["L0_rec_b0"], a["L0_rec_b1"][swap], a["L0_rec_b2"]], axis=1),
        "wt1": np.concatenate([wt1[HALF:S], wt1[:HALF], wt1[S:]], axis=0),
        "bt1": a["b_top1"].reshape(-1, P).T,
        "wt2": a["W_top2"],
        "bt2": a["b_top2"].reshape(-1, P).T,
        "wt3": a["W_top3"].reshape(-1, P).T,
        "ctxT": a["dense_ctx"].T,
    }
    for f in range(F):
        arrays[f"tbl_{f}"] = a[f"tbl_{f}"]
    arrays = {f"{k}_dram": np.ascontiguousarray(v) for k, v in arrays.items()}
    nc = bacc.Bacc("TRN2", target_bir_lowering=False, num_devices=1)
    ap = {k: nc.dram_tensor(k, v.shape, mybir.dt.from_np(v.dtype), kind="ExternalInput").ap()
          for k, v in arrays.items()}
    out = nc.dram_tensor("out_dram", (B, 1), F32, kind="ExternalOutput").ap()
    tower_kernel(nc, ap["ids_dram"], [ap[f"tbl_{f}_dram"] for f in range(F)],
                 *[ap[f"{k}_dram"] for k in ("sel", "ident", "w0a", "w0b", "w1", "w2", "biases",
                                             "wt1", "bt1", "wt2", "bt2", "wt3", "ctxT")], out)
    r = run_bass_kernel_spmd(nc, [arrays], core_ids=[0])
    return r.results[0]["out_dram"]
```
